# Optimizing a Trainium2 kernel written in Bass

```python
import numpy as np
import jax
import jax.numpy as jnp

def _softmax(x, axis=-1):
    return jax.nn.softmax(x, axis=axis)

def _gelu(x):
    return jax.nn.gelu(x, approximate=True)

def _silu(x):
    return jax.nn.silu(x)

def _sigmoid(x):
    return jax.nn.sigmoid(x)

def _layernorm(x, axis=-1, eps=1e-05):
    m = jnp.mean(x, axis=axis, keepdims=True)
    v = jnp.var(x, axis=axis, keepdims=True)
    return (x - m) / jnp.sqrt(v + eps)

def _scatter_add(tgt, idx, src, axis=0):
    return tgt.at[idx].add(src)

def _segment_sum(src, seg, n):
    return jax.ops.segment_sum(src, seg, n)
kernel_name = 'mk_metaformer_d1_conv_nhwc512_r4_e845f2'

def setup_inputs(seed: int=0):
    np.random.seed(seed)
    _w = jnp.asarray

    def _rec_inputs():
        import jax
        import jax.numpy as jnp
        _gk = jax.random.key(seed)
        x = -0.000125 + 0.9999 * jax.random.normal(jax.random.fold_in(_gk, 1), (4, 32, 32, 128), jnp.float32)
        return x
    x = _rec_inputs()

    def _L0_conv_setup():
        import jax, jax.numpy as jnp
        import numpy as np
        DIM = 128
        HEADS = 16
        HD = DIM // HEADS
        WH, WW = (8, 8)
        D0, D1 = (2, 2)
        TWH, TWW = (WH * D0, WW * D1)
        SCALE = HD ** (-0.5)

        def _wpart(x, wh, ww):
            B, H, W, C = x.shape
            x = x.reshape(B, H // wh, wh, W // ww, ww, C)
            return x.transpose(0, 1, 3, 2, 4, 5).reshape(-1, wh, ww, C)

        def _wrev(win, wh, ww, H, W):
            C = win.shape[-1]
            B = win.shape[0] // (H // wh * (W // ww))
            x = win.reshape(B, H // wh, W // ww, wh, ww, C).transpose(0, 1, 3, 2, 4, 5)
            return x.reshape(B, H, W, C)

        def _rope2(x):
            d = HD // 2
            inv = 1.0 / 10000.0 ** (jnp.arange(0, d, 2, dtype=jnp.float32) / d)

            def rot(xp, ang):
                x1, x2 = (xp[..., 0::2], xp[..., 1::2])
                c, s = (jnp.cos(ang), jnp.sin(ang))
                return jnp.stack([x1 * c - x2 * s, x1 * s + x2 * c], axis=-1).reshape(xp.shape)
            ah = (jnp.arange(WH, dtype=jnp.float32)[:, None] * inv)[:, None, :]
            aw = (jnp.arange(WW, dtype=jnp.float32)[:, None] * inv)[None, :, :]
            return jnp.concatenate([rot(x[..., :d], ah), rot(x[..., d:], aw)], axis=-1)

        def _forward(x, qkv_w, qkv_b, proj_w, proj_b):
            B, H, W, C = x.shape
            xw = _wpart(x, TWH, TWW)
            B_ = xw.shape[0]
            xw = _wpart(xw, D0, D1)
            xw = xw.reshape(B_, WH * WW, D0 * D1, C)
            xw = xw.transpose(0, 2, 1, 3).reshape(B_ * D0 * D1, WH * WW, C)
            B__, N = (xw.shape[0], xw.shape[1])
            qkv = (xw @ qkv_w.T + qkv_b).reshape(B__, N, 3, HEADS, HD).transpose(2, 0, 3, 1, 4)
            q, k, v = (qkv[0], qkv[1], qkv[2])
            q = _rope2(q.reshape(-1, WH, WW, HD)).reshape(B__, HEADS, N, HD) * SCALE
            k = _rope2(k.reshape(-1, WH, WW, HD)).reshape(B__, HEADS, N, HD)
            attn = jax.nn.softmax(jnp.einsum('bhnd,bhmd->bhnm', q, k), axis=-1)
            out = jnp.einsum('bhnm,bhmd->bhnd', attn, v)
            out = out.transpose(0, 2, 1, 3).reshape(B__, N, C)
            out = out.reshape(B_, D0 * D1, N, C).transpose(0, 2, 1, 3).reshape(-1, D0, D1, C)
            out = _wrev(out, D0, D1, TWH, TWW)
            out = _wrev(out, TWH, TWW, H, W)
            return out @ proj_w.T + proj_b
        key = jax.random.key(seed)
        k0, k1, k2 = jax.random.split(key, 3)
        x = jax.random.normal(k0, (4, 32, 32, DIM), dtype=jnp.float32)
        qkv_w = jax.random.normal(k1, (3 * DIM, DIM), dtype=jnp.float32) * DIM ** (-0.5)
        qkv_b = jnp.zeros((3 * DIM,), dtype=jnp.float32)
        proj_w = jax.random.normal(k2, (DIM, DIM), dtype=jnp.float32) * DIM ** (-0.5)
        proj_b = jnp.zeros((DIM,), dtype=jnp.float32)
        return {'x': x, 'qkv_w': qkv_w, 'qkv_b': qkv_b, 'proj_w': proj_w, 'proj_b': proj_b}
    _L0_conv_all = _L0_conv_setup()
    _L0_conv_in = {k: v for k, v in _L0_conv_all.items() if k in ('qkv_w', 'qkv_b', 'proj_w', 'proj_b')}
    del _L0_conv_all

    def _L0_ffn_setup():
        import jax, jax.numpy as jnp
        import numpy as np
        B, S, D, F, E, NS, K = (2, 512, 128, 512, 8, 2, 2)
        key = jax.random.key(seed)
        ks = jax.random.split(key, 6)
        scale = 0.02

        def p(k, shape):
            return jax.random.normal(k, shape, jnp.float32) * scale
        return {'x': jax.random.normal(ks[0], (B, S, D), jnp.float32), 'gate_w': p(ks[1], (E, D)), 'gate_b': jnp.zeros((E,), jnp.float32), 'sw1': p(ks[2], (NS, F, D)), 'sb1': jnp.zeros((NS, F), jnp.float32), 'sw2': p(ks[3], (NS, D, F)), 'sb2': jnp.zeros((NS, D), jnp.float32), 'rw1': p(ks[4], (E, F, D)), 'rb1': jnp.zeros((E, F), jnp.float32), 'rw2': p(ks[5], (E, D, F)), 'rb2': jnp.zeros((E, D), jnp.float32)}
    _L0_ffn_all = _L0_ffn_setup()
    _L0_ffn_in = {k: v for k, v in _L0_ffn_all.items() if k in ('gate_w', 'gate_b', 'sw1', 'sb1', 'sw2', 'sb2', 'rw1', 'rb1', 'rw2', 'rb2')}
    del _L0_ffn_all
    return {'x': x, 'L0_conv_qkv_w': _L0_conv_in['qkv_w'], 'L0_conv_qkv_b': _L0_conv_in['qkv_b'], 'L0_conv_proj_w': _L0_conv_in['proj_w'], 'L0_conv_proj_b': _L0_conv_in['proj_b'], 'L0_ffn_gate_w': _L0_ffn_in['gate_w'], 'L0_ffn_gate_b': _L0_ffn_in['gate_b'], 'L0_ffn_sw1': _L0_ffn_in['sw1'], 'L0_ffn_sb1': _L0_ffn_in['sb1'], 'L0_ffn_sw2': _L0_ffn_in['sw2'], 'L0_ffn_sb2': _L0_ffn_in['sb2'], 'L0_ffn_rw1': _L0_ffn_in['rw1'], 'L0_ffn_rb1': _L0_ffn_in['rb1'], 'L0_ffn_rw2': _L0_ffn_in['rw2'], 'L0_ffn_rb2': _L0_ffn_in['rb2']}

def reference(x, L0_conv_qkv_w, L0_conv_qkv_b, L0_conv_proj_w, L0_conv_proj_b, L0_ffn_gate_w, L0_ffn_gate_b, L0_ffn_sw1, L0_ffn_sb1, L0_ffn_sw2, L0_ffn_sb2, L0_ffn_rw1, L0_ffn_rb1, L0_ffn_rw2, L0_ffn_rb2):
    import jax
    import jax.numpy as jnp

    def _L0_conv_ref(x, qkv_w, qkv_b, proj_w, proj_b):
        import jax, jax.numpy as jnp
        import numpy as np
        DIM = 128
        HEADS = 16
        HD = DIM // HEADS
        WH, WW = (8, 8)
        D0, D1 = (2, 2)
        TWH, TWW = (WH * D0, WW * D1)
        SCALE = HD ** (-0.5)

        def _wpart(x, wh, ww):
            B, H, W, C = x.shape
            x = x.reshape(B, H // wh, wh, W // ww, ww, C)
            return x.transpose(0, 1, 3, 2, 4, 5).reshape(-1, wh, ww, C)

        def _wrev(win, wh, ww, H, W):
            C = win.shape[-1]
            B = win.shape[0] // (H // wh * (W // ww))
            x = win.reshape(B, H // wh, W // ww, wh, ww, C).transpose(0, 1, 3, 2, 4, 5)
            return x.reshape(B, H, W, C)

        def _rope2(x):
            d = HD // 2
            inv = 1.0 / 10000.0 ** (jnp.arange(0, d, 2, dtype=jnp.float32) / d)

            def rot(xp, ang):
                x1, x2 = (xp[..., 0::2], xp[..., 1::2])
                c, s = (jnp.cos(ang), jnp.sin(ang))
                return jnp.stack([x1 * c - x2 * s, x1 * s + x2 * c], axis=-1).reshape(xp.shape)
            ah = (jnp.arange(WH, dtype=jnp.float32)[:, None] * inv)[:, None, :]
            aw = (jnp.arange(WW, dtype=jnp.float32)[:, None] * inv)[None, :, :]
            return jnp.concatenate([rot(x[..., :d], ah), rot(x[..., d:], aw)], axis=-1)

        def _forward(x, qkv_w, qkv_b, proj_w, proj_b):
            B, H, W, C = x.shape
            xw = _wpart(x, TWH, TWW)
            B_ = xw.shape[0]
            xw = _wpart(xw, D0, D1)
            xw = xw.reshape(B_, WH * WW, D0 * D1, C)
            xw = xw.transpose(0, 2, 1, 3).reshape(B_ * D0 * D1, WH * WW, C)
            B__, N = (xw.shape[0], xw.shape[1])
            qkv = (xw @ qkv_w.T + qkv_b).reshape(B__, N, 3, HEADS, HD).transpose(2, 0, 3, 1, 4)
            q, k, v = (qkv[0], qkv[1], qkv[2])
            q = _rope2(q.reshape(-1, WH, WW, HD)).reshape(B__, HEADS, N, HD) * SCALE
            k = _rope2(k.reshape(-1, WH, WW, HD)).reshape(B__, HEADS, N, HD)
            attn = jax.nn.softmax(jnp.einsum('bhnd,bhmd->bhnm', q, k), axis=-1)
            out = jnp.einsum('bhnm,bhmd->bhnd', attn, v)
            out = out.transpose(0, 2, 1, 3).reshape(B__, N, C)
            out = out.reshape(B_, D0 * D1, N, C).transpose(0, 2, 1, 3).reshape(-1, D0, D1, C)
            out = _wrev(out, D0, D1, TWH, TWW)
            out = _wrev(out, TWH, TWW, H, W)
            return out @ proj_w.T + proj_b
        return _forward(x, qkv_w, qkv_b, proj_w, proj_b)

    def _L0_ffn_ref(x, gate_w, gate_b, sw1, sb1, sw2, sb2, rw1, rb1, rw2, rb2):
        import jax, jax.numpy as jnp
        import numpy as np
        B, S, D, F, E, NS, K = (2, 512, 128, 512, 8, 2, 2)
        b, s, d = x.shape
        t = x.reshape(-1, d)
        T = t.shape[0]
        hs = jax.nn.gelu(jnp.einsum('td,nfd->ntf', t, sw1) + sb1[:, None, :], approximate=False)
        shared = jnp.einsum('ntf,ndf->td', hs, sw2) + sb2.sum(axis=0)
        logits = t @ gate_w.T + gate_b
        probs = jax.nn.softmax(logits, axis=-1)
        top_v, top_i = jax.lax.top_k(probs, K)
        cw = jnp.zeros_like(probs).at[jnp.arange(T)[:, None], top_i].add(top_v)
        hr = jax.nn.gelu(jnp.einsum('td,efd->etf', t, rw1) + rb1[:, None, :], approximate=False)
        oe = jnp.einsum('etf,edf->etd', hr, rw2) + rb2[:, None, :]
        routed = jnp.einsum('etd,te->td', oe, cw)
        return (shared + routed).reshape(b, s, d)

    def _gn(v, G=32, eps=1e-05):
        B_, H_, W_, C_ = v.shape
        g = v.reshape(B_, H_, W_, G, C_ // G)
        m = jnp.mean(g, axis=(1, 2, 4), keepdims=True)
        s = jnp.var(g, axis=(1, 2, 4), keepdims=True)
        return ((g - m) / jnp.sqrt(s + eps)).reshape(v.shape)

    def _ln_c(v, eps=1e-06):
        m = jnp.mean(v, axis=-1, keepdims=True)
        s = jnp.var(v, axis=-1, keepdims=True)
        return (v - m) / jnp.sqrt(s + eps)

    def _ln_t(v, eps=1e-05):
        m = jnp.mean(v, axis=-1, keepdims=True)
        s = jnp.var(v, axis=-1, keepdims=True)
        return (v - m) / jnp.sqrt(s + eps)

    def _to_tokens(v):
        B_, H_, W_, C_ = v.shape
        return v.reshape(B_, H_ * W_, C_)

    def _from_tokens(t, like):
        return t.reshape(like.shape)
    x = x + _L0_conv_ref(_ln_c(x), L0_conv_qkv_w, L0_conv_qkv_b, L0_conv_proj_w, L0_conv_proj_b)
    t = _to_tokens(x)
    t = t + _L0_ffn_ref(_ln_t(t), L0_ffn_gate_w, L0_ffn_gate_b, L0_ffn_sw1, L0_ffn_sb1, L0_ffn_sw2, L0_ffn_sb2, L0_ffn_rw1, L0_ffn_rb1, L0_ffn_rw2, L0_ffn_rb2)
    x = _from_tokens(t, x)
    return x

_drawn_inputs = setup_inputs


def setup_inputs(seed=0):
    import zlib

    import numpy as np

    out = dict(_drawn_inputs(seed))
    spreads = {'L0_conv_qkv_b': (0.0, 0.1),
     'L0_conv_proj_b': (0.0, 0.1),
     'L0_ffn_gate_b': (0.0, 0.451),
     'L0_ffn_sb1': (0.0, 0.285),
     'L0_ffn_sb2': (0.0, 0.1),
     'L0_ffn_rb1': (0.0, 0.8),
     'L0_ffn_rb2': (0.0, 0.337)}
    factors = {'L0_ffn_rw1': 4.693, 'L0_ffn_rw2': 4.186}
    for name, (base, spread) in spreads.items():
        noise = np.random.default_rng([zlib.crc32(name.encode()), seed]).standard_normal(out[name].shape)
        drawn = base * np.exp(spread * noise) if base else spread * noise
        out[name] = jnp.asarray(drawn.astype(out[name].dtype))
    for name, factor in factors.items():
        out[name] = (out[name] * factor).astype(out[name].dtype)
    return out
```

```python
from contextlib import ExitStack

import numpy as np

import concourse.bass as bass
from concourse import mybir

F32 = mybir.dt.float32
F32R = mybir.dt.float32r
BF16 = mybir.dt.bfloat16
ALU = mybir.AluOpType
ACT = mybir.ActivationFunctionType
AX = mybir.AxisListType

P = 128
C = 128
TOKENS = 4096
TILE = 512
TILES = TOKENS // TILE
SUBS = TILE // P
WIN = 64
SEQS = TILE // WIN
HEADS, HD = 16, 8
SCALE = HD ** -0.5
HPR = 4
UNITS = 4
SHARED, ROUTED, TOPK = 2, 8, 2
EXPERTS = SHARED + ROUTED
FC = 4
CHUNKS = EXPERTS * FC
CW_ROWS = 3 * ROUTED + SHARED
EPS_CONV, EPS_FFN = 1e-6, 1e-5
MIN_NORMAL = 1.1754944e-38
W_COLS = 2 * CHUNKS * P
W_PER_TILE = 2
W_BLOCK = W_COLS // (TILES * W_PER_TILE)

QKV_BLOCKS = 6
CONST_COLS = {"ident": P, "cos": WIN, "sin": WIN, "headmask": HPR, "tiebreak": SUBS * ROUTED * ROUTED}
BIAS_COLS = {"q": 1, "qs": 1, "k": 1, "ks": 1, "v": 1, "b1": CHUNKS}


def offsets(cols):
    at, out = 0, {}
    for name, n in cols.items():
        out[name] = slice(at, at + n)
        at += n
    return out, at


CONST_AT, CONST_N = offsets(CONST_COLS)
BIAS_AT, BIAS_N = offsets(BIAS_COLS)


def at(tile, per_tile, k):
    return tile * per_tile + k


def wait(eng, sem, value):
    if isinstance(value, int) and value <= 0:
        return
    eng.wait_ge(sem, value)


def tile_of(tensor, n):
    if isinstance(n, int):
        return tensor[n]
    return tensor[bass.ds(n, 1), :, :].rearrange("o p n -> p (o n)")


def shared_bank_uses(closing, opening):
    order = (["proj", "x2T", "xn2T", "gate"] if closing else []) + (["xnT"] if opening else [])
    order += (["q"] if opening else []) + (["qs"] if opening else [])
    order += (["cwT"] if closing else [])
    order += (["k", "ks", "v0", "v1"] if opening else [])
    return {name: n for n, name in enumerate(order)}, len(order)


def attention_phase(nc, d, keep):
    with ExitStack() as ctx:
        def sb(name, shape, dt=F32):
            return ctx.enter_context(nc.sbuf_tensor(name, shape, dt))

        def psum(name, shape):
            return ctx.enter_context(nc.psum_tensor(name, shape, F32))

        def sem(name):
            return ctx.enter_context(nc.semaphore(name))

        scores_ps = [psum(f"scores_ps{i}", [P, 1024]) for i in range(2)]
        probsT_ps = [psum(f"probsT_ps{i}", [P, 512]) for i in range(2)]
        attn_ps = psum("attn_ps", [P, 512])
        shared_ps = psum("shared_ps", [P, 512])

        wqkv = sb("wqkv", [P, QKV_BLOCKS * P])
        gate_w = sb("gate_w", [P, ROUTED])
        gate_b = sb("gate_b", [P, SUBS * ROUTED])
        proj_b = sb("proj_b", [P, TILE])
        half_neg = sb("half_neg", [P, SUBS])
        x_in = sb("x_in", [P, TILE])
        x_res = sb("x_res", [P, TILE])
        stats = sb("stats", [P, SUBS, 6])
        stats2 = sb("stats2", [P, SUBS, 6])
        mv1, mv2 = sb("mv1", [P, SUBS, 2]), sb("mv2", [P, SUBS, 2])
        ve1, ve2 = sb("ve1", [P, SUBS]), sb("ve2", [P, SUBS])
        rstd1, rstd2 = sb("rstd1", [P, SUBS]), sb("rstd2", [P, SUBS])
        eps_conv, eps_ffn = sb("eps_conv", [P, SUBS]), sb("eps_ffn", [P, SUBS])
        xn, xn2 = sb("xn", [P, TILE]), sb("xn2", [P, TILE])
        xnT = sb("xnT", [P, TILE])
        xn2T_now = sb("xn2T_now", [P, TILE])
        q_cos, q_sin = sb("q_cos", [P, TILE]), sb("q_sin", [P, TILE])
        k_cos, k_sin = sb("k_cos", [P, TILE]), sb("k_sin", [P, TILE])
        q_rot, k_rot = sb("q_rot", [P, TILE]), sb("k_rot", [P, TILE])
        k_masked = sb("k_masked", [P, SEQS, HPR, WIN])
        v_spread = sb("v_spread", [P, SEQS * (HEADS // 2) * 32 + 32])
        smax = sb("smax", [P, 2, 16])
        shifted = [sb(f"shifted{i}", [P, 1024]) for i in range(2)]
        probs = [sb(f"probs{i}", [P, 1024]) for i in range(2)]
        psums, rinv = sb("psums", [P, 2, 16]), sb("rinv", [P, 2, 16])
        probsT = [sb(f"probsT{i}", [P, 4, P]) for i in range(2)]
        attnT = sb("attnT", [P, TILE])
        x2 = sb("x2", [P, TILE])
        G = [P, SUBS, ROUTED]
        logits, lshift, lexp = sb("logits", G), sb("lshift", G), sb("lexp", G)
        lmax, lsum, linv = (sb(n, [P, SUBS]) for n in ("lmax", "lsum", "linv"))
        pairdiff = sb("pairdiff", [P, SUBS, ROUTED, ROUTED])
        beats = sb("beats", [P, SUBS, ROUTED, ROUTED])
        rank, chosen, cw, cw_rest = sb("rank", G), sb("chosen", G), sb("cw", G), sb("cw_rest", G)
        zeros = sb("zeros", G)
        cw_parts = sb("cw_parts", [P, SUBS, CW_ROWS], BF16)
        ident_bf = sb("ident_bf", [P, P], BF16)
        w_stage = sb("w_stage", [P, W_PER_TILE, W_BLOCK])

        weights_in = sem("weights_in")
        x_loaded, xres_loaded = sem("x_loaded"), sem("xres_loaded")
        pool_fills, dve_casts = sem("pool_fills"), sem("dve_casts")
        ln1_done, rstd1_step, xn_ready = sem("ln1_done"), sem("rstd1_step"), sem("xn_ready")
        ln2_done, rstd2_step, xn2_ready = sem("ln2_done"), sem("rstd2_step"), sem("xn2_ready")
        stat_step = sem("stat_step")
        bank_written, bank_read = sem("bank_written"), sem("bank_read")
        q_ready, k_ready, k_masked_ready = sem("q_ready"), sem("k_ready"), sem("k_masked_ready")
        scores_done, max_done, shifted_ready = sem("scores_done"), sem("max_done"), sem("shifted_ready")
        probs_ready, sum_done, rinv_ready = sem("probs_ready"), sem("sum_done"), sem("rinv_ready")
        normed, transposed, probsT_ready = sem("normed"), sem("transposed"), sem("probsT_ready")
        pv_half, pv_done, attnT_ready = sem("pv_half"), sem("pv_done"), sem("attnT_ready")
        xres_biased, x2_ready = sem("xres_biased"), sem("x2_ready")
        gate_step, lexp_ready, cw_ready = sem("gate_step"), sem("lexp_ready"), sem("cw_ready")
        parts_step = sem("parts_step")
        w_loaded = [sem(f"w_loaded{j}") for j in range(W_PER_TILE)]
        w_hi_ready, w_lo_ready = sem("w_hi_ready"), sem("w_lo_ready")

        ident = keep["const"][:, CONST_AT["ident"]]
        cos = keep["const"][:, CONST_AT["cos"]]
        sin = keep["const"][:, CONST_AT["sin"]]
        headmask = keep["const"][:, CONST_AT["headmask"]]
        tiebreak = keep["const"][:, CONST_AT["tiebreak"]]

        def bias(name):
            return keep["bias"][:, BIAS_AT[name]]

        SETUP_DMAS = 8
        POOL_FILLS = 6
        DVE_CASTS = 6

        def w_block(which, n):
            return which[:, bass.ds(n * W_BLOCK, W_BLOCK)]

        GATE_STEPS, LSHIFT, CW_FIRST = 10, 3, 10

        def run_iterations(eng, body):
            closing_uses, opening_uses = shared_bank_uses(True, False)[1], shared_bank_uses(False, True)[1]
            uses = closing_uses + opening_uses
            first = 2 * opening_uses - uses
            body(-1, 0, False, True, units=False)
            body(0, opening_uses, False, True)
            with eng.Fori(1, TILES - 1) as t:
                body(t, t * uses + first, True, True)
            body(TILES - 1, (TILES - 1) * uses + first, True, False)
            body(TILES, (TILES - 1) * uses + first + closing_uses, True, False, units=False)

        block = ctx.enter_context(nc.Block())

        @block.sync
        def _(sp):
            sp.dma_start(x_in[:], d["x"][0]).then_inc(x_loaded, 16)
            sp.dma_start(keep["const"][:], d["const"]).then_inc(weights_in, 16)
            sp.dma_start(wqkv[:], d["wqkv"]).then_inc(weights_in, 16)
            sp.dma_start(keep["bias"][:], d["bias"]).then_inc(weights_in, 16)
            sp.dma_start(gate_w[:], d["gate_w"]).then_inc(weights_in, 16)
            sp.dma_start(gate_b[:], d["gate_b"]).then_inc(weights_in, 16)
            sp.dma_start(proj_b[:], d["proj_b"]).then_inc(weights_in, 16)
            sp.dma_start(keep["b2"][:], d["b2"]).then_inc(weights_in, 16)
            sp.dma_start(probs[1][0:CW_ROWS, :], d["sel"]).then_inc(weights_in, 16)
            sp.dma_start(x_res[:], d["x"][0]).then_inc(xres_loaded, 16)

            def w_loads(t):
                for j in range(W_PER_TILE):
                    wait(sp, w_lo_ready, at(t, W_PER_TILE, j + 1 - W_PER_TILE))
                    sp.dma_start(w_stage[:, j, :], tile_of(d["w12"], t * W_PER_TILE + j)).then_inc(w_loaded[j], 16)

            def body(t, closing, opening):
                if opening:
                    wait(sp, xn_ready, at(t, 1, 1))
                    sp.dma_start(x_in[:], tile_of(d["x"], t + 1)).then_inc(x_loaded, 16)
                w_loads(t)
                if closing:
                    wait(sp, x2_ready, at(t, 1, 0))
                    sp.dma_start(x_res[:], tile_of(d["x"], t)).then_inc(xres_loaded, 16)

            body(0, False, True)
            with sp.Fori(1, TILES - 1) as t:
                body(t, True, True)
            body(TILES - 1, True, False)

        @block.tensor
        def _(pe):
            def into_shared_bank(n):
                wait(pe, bank_read, n)

            def transposes(src, n):
                into_shared_bank(n)
                for s in range(SUBS):
                    mm = nc.tensor.transpose(shared_ps[:, s * P:(s + 1) * P], src[:, s * P:(s + 1) * P], ident)
                mm.then_inc(bank_written, 1)

            def open_xnT(t, n):
                wait(pe, xn_ready, at(t, 1, 1))
                transposes(xn, n)

            def open_qk(b, n):
                into_shared_bank(n)
                nc.tensor.matmul(shared_ps[:], wqkv[:, b * P:(b + 1) * P], xnT[:],
                                 start=True, stop=True).then_inc(bank_written, 1)

            def open_v(quad, n):
                into_shared_bank(n)
                for s in range(4):
                    seq = quad * 4 + s
                    for h2 in range(2):
                        mm = nc.tensor.matmul(shared_ps[64 * h2:64 * h2 + 64, s * P:(s + 1) * P],
                                              xnT[:, seq * WIN:(seq + 1) * WIN],
                                              wqkv[:, 4 * P:5 * P], start=True, stop=True)
                mm.then_inc(bank_written, 1)

            def scores(t, u):
                quad, half = divmod(u, 2)
                if u == 0:
                    wait(pe, q_ready, at(t, 1, 1))
                    wait(pe, k_masked_ready, at(t, 1, 1))
                wait(pe, shifted_ready, at(t, UNITS, u - 1))
                for pair in range(2):
                    for i in range(2):
                        for s in range(2):
                            seq, rg = quad * 4 + pair * 2 + s, 2 * half + i
                            rows = slice(32 * rg, 32 * rg + 32)
                            mm = nc.tensor.matmul(
                                scores_ps[u % 2][64 * s:64 * s + 64, i * 512 + pair * 256:i * 512 + pair * 256 + 256],
                                q_rot[rows, seq * WIN:(seq + 1) * WIN],
                                k_masked[rows, seq, :, :].rearrange("p h m -> p (h m)"), start=True, stop=True)
                mm.then_inc(scores_done, 1)

            def probs_transposes(t, u):
                wait(pe, normed, at(t, UNITS, u + 1))
                for pair in range(2):
                    wait(pe, probsT_ready, at(t, 2 * UNITS, 2 * u + pair - 1))
                    for b in range(4):
                        i, h2 = divmod(b, 2)
                        c0 = i * 512 + pair * 256 + h2 * P
                        mm = nc.tensor.transpose(probsT_ps[pair][:, b * P:(b + 1) * P],
                                                 probs[u % 2][:, c0:c0 + P], ident)
                    mm.then_inc(transposed, 1)

            def values(t, u, m0):
                quad, half = divmod(u, 2)
                wait(pe, attnT_ready, at(t, UNITS, u))
                if u == 0:
                    wait(pe, bank_read, m0)
                for pair in range(2):
                    wait(pe, probsT_ready, at(t, 2 * UNITS, 2 * u + pair + 1))
                    for s in range(2):
                        for h2 in range(2):
                            for i in range(2):
                                rg, seq = 2 * half + i, quad * 4 + pair * 2 + s
                                c0 = (seq * (HEADS // 2) + 2 * rg + h2) * 32 - 16 * h2
                                col = (pair * 2 + s) * WIN
                                mm = nc.tensor.matmul(
                                    attn_ps[32 * rg:32 * rg + 32, col:col + WIN],
                                    v_spread[:, 16 + c0:16 + c0 + 32],
                                    probsT[pair][:, 2 * i + h2, s * WIN:(s + 1) * WIN],
                                    start=(h2 == 0), stop=(h2 == 1), skip_group_check=True)
                    if pair == 0:
                        mm.then_inc(pv_half, 1)
                mm.then_inc(pv_done, 1)

            def close_proj(t, n):
                wait(pe, attnT_ready, at(t, UNITS, UNITS))
                into_shared_bank(n)
                for s in range(SUBS):
                    mm = nc.tensor.matmul(shared_ps[:, s * P:(s + 1) * P], attnT[:, s * P:(s + 1) * P],
                                          wqkv[:, 5 * P:6 * P], start=True, stop=True)
                mm.then_inc(bank_written, 1)

            def close_gate(t, n):
                into_shared_bank(n)
                for s in range(SUBS):
                    mm = nc.tensor.matmul(shared_ps[:, s * ROUTED:(s + 1) * ROUTED], xn2T_now[:, s * P:(s + 1) * P],
                                          gate_w[:], start=True, stop=True)
                mm.then_inc(bank_written, 1)

            def close_cwT(t, n):
                wait(pe, cw_ready, at(t, 1, 1))
                into_shared_bank(n)
                for s in range(SUBS):
                    mm = nc.tensor.transpose(shared_ps[:].bitcast(BF16)[0:CW_ROWS, s * P:(s + 1) * P],
                                             cw_parts[:, s, :], ident_bf[:])
                mm.then_inc(bank_written, 1)

            def body(t, m0, closing, opening, units=True):
                use, _n = shared_bank_uses(closing, opening)
                at_bank = {k: m0 + v for k, v in use.items()}
                if units:
                    scores(t, 0)
                    scores(t, 1)
                if closing:
                    close_proj(t - 1, at_bank["proj"])
                if units:
                    probs_transposes(t, 0)
                if closing:
                    wait(pe, x2_ready, at(t - 1, 1, 1))
                    transposes(x2, at_bank["x2T"])
                if units:
                    values(t, 0, m0)
                    scores(t, 2)
                if closing:
                    wait(pe, xn2_ready, at(t - 1, 1, 1))
                    transposes(xn2, at_bank["xn2T"])
                if units:
                    probs_transposes(t, 1)
                if closing:
                    close_gate(t - 1, at_bank["gate"])
                if units:
                    values(t, 1, m0)
                    scores(t, 3)
                if opening:
                    open_xnT(t + 1, at_bank["xnT"])
                if units:
                    probs_transposes(t, 2)
                if opening:
                    open_qk(0, at_bank["q"])
                if units:
                    values(t, 2, m0)
                if opening:
                    open_qk(1, at_bank["qs"])
                if closing:
                    close_cwT(t - 1, at_bank["cwT"])
                if units:
                    probs_transposes(t, 3)
                if opening:
                    open_qk(2, at_bank["k"])
                if units:
                    values(t, 3, m0)
                if opening:
                    open_qk(3, at_bank["ks"])
                    open_v(0, at_bank["v0"])
                    open_v(1, at_bank["v1"])

            pe.wait_ge(weights_in, 16 * SETUP_DMAS)
            pe.wait_ge(pool_fills, POOL_FILLS)
            pe.wait_ge(dve_casts, DVE_CASTS)
            run_iterations(pe, body)

        @block.scalar
        def _(act):
            def from_bank(n, out, inp):
                wait(act, bank_written, n + 1)
                nc.scalar.copy(out, inp).then_inc(bank_read, 1)

            def exp(t, u):
                wait(act, shifted_ready, at(t, UNITS, u + 1))
                wait(act, transposed, at(t, 2 * UNITS, 2 * (u - 1)))
                nc.scalar.activation(probs[u % 2][:], shifted[u % 2][:], ACT.Exp, scale=SCALE).then_inc(probs_ready, 1)

            def copy_probsT(t, u):
                for pair in range(2):
                    wait(act, transposed, at(t, 2 * UNITS, 2 * u + pair + 1))
                    wait(act, pv_half if pair == 0 else pv_done, at(t, UNITS, u))
                    nc.scalar.copy(probsT[pair][:].rearrange("p b n -> p (b n)"), probsT_ps[pair][:]).then_inc(probsT_ready, 1)

            def copy_attn(t, u):
                quad, half = divmod(u, 2)
                rows = slice(64 * half, 64 * half + 64)
                wait(act, pv_done, at(t, UNITS, u + 1))
                if u == 0:
                    wait(act, x2_ready, at(t, 1, 0))
                nc.scalar.activation(attnT[rows, quad * 256:quad * 256 + 256], attn_ps[rows, 0:256], ACT.Identity,
                                     bias=bias("v")[rows, :]).then_inc(attnT_ready, 1)

            def mask_k(t):
                wait(act, k_ready, at(t, 1, 1))
                wait(act, scores_done, at(t, UNITS, 0))
                for h in range(HPR):
                    op = nc.scalar.mul(k_masked[:, :, h, :], k_rot[:].rearrange("p (s m) -> p s m", s=SEQS),
                                       headmask[:, h:h + 1])
                op.then_inc(k_masked_ready, 1)

            def spread_v(t, quad, n):
                wait(act, bank_written, n + 1)
                wait(act, pv_done, at(t, UNITS, 0))
                for h2 in range(2):
                    rows = slice(64 * h2, 64 * h2 + 64)
                    groups = 4 * HEADS // 2
                    dst = v_spread[rows, 16 + quad * groups * 32:16 + (quad + 1) * groups * 32].rearrange(
                        "p (g w) -> p g w", w=32)[:, :, h2 * HD:(h2 + 1) * HD]
                    src = shared_ps[rows, :].rearrange("p (g w) -> p g w", w=16)[:, :, h2 * HD:(h2 + 1) * HD]
                    op = nc.scalar.copy(dst, src)
                op.then_inc(bank_read, 1)

            def split_w_hi(t):
                for j in range(W_PER_TILE):
                    wait(act, w_loaded[j], at(t, 16, 16))
                    nc.scalar.copy(w_block(keep["w_hi"], t * W_PER_TILE + j), w_stage[:, j, :]).then_inc(w_hi_ready, 1)

            def body(t, m0, closing, opening, units=True):
                use, _n = shared_bank_uses(closing, opening)
                b = {k: m0 + v for k, v in use.items()}
                if units:
                    exp(t, 0)
                    exp(t, 1)
                if closing:
                    from_bank(b["x2T"], keep["x2T"][:, bass.ds((t - 1) * TILE, TILE)], shared_ps[:])
                if units:
                    copy_probsT(t, 0)
                    copy_attn(t, 0)
                    exp(t, 2)
                if closing:
                    wait(act, bank_written, b["xn2T"] + 1)
                    nc.scalar.copy(keep["xn2T"][:, bass.ds((t - 1) * TILE, TILE)], shared_ps[:])
                    nc.scalar.copy(xn2T_now[:], shared_ps[:]).then_inc(bank_read, 1)
                if units:
                    copy_probsT(t, 1)
                if closing:
                    wait(act, gate_step, at(t - 1, GATE_STEPS, LSHIFT))
                    nc.scalar.activation(lexp[:], lshift[:], ACT.Exp).then_inc(lexp_ready, 1)
                if units:
                    copy_attn(t, 1)
                    exp(t, 3)
                if opening:
                    from_bank(b["xnT"], xnT[:], shared_ps[:])
                if units:
                    copy_probsT(t, 2)
                    copy_attn(t, 2)
                if closing:
                    wait(act, bank_written, b["cwT"] + 1)
                    nc.scalar.copy(keep["cwT"][0:CW_ROWS, bass.ds((t - 1) * TILE, TILE)],
                                   shared_ps[:].bitcast(BF16)[0:CW_ROWS, 0:TILE]).then_inc(bank_read, 1)
                if units:
                    copy_probsT(t, 3)
                    copy_attn(t, 3)
                if opening:
                    mask_k(t + 1)
                    spread_v(t + 1, 0, b["v0"])
                    spread_v(t + 1, 1, b["v1"])
                if units:
                    split_w_hi(t)

            act.wait_ge(weights_in, 16 * SETUP_DMAS)
            act.wait_ge(pool_fills, POOL_FILLS)
            run_iterations(act, body)

        @block.vector
        def _(dve):
            def row_stats(src, raw, begun=None):
                for s in range(SUBS):
                    op = nc.vector.bn_stats(raw[:, s, :], src[:, s * P:(s + 1) * P])
                    if s == 0 and begun is not None:
                        op.then_inc(begun, 1)
                op.then_inc(stat_step, 1)

            def merge_stats(raw, mv, done):
                for s in range(SUBS):
                    op = nc.vector.bn_aggr(mv[:, s, :], raw[:, s, :])
                op.then_inc(done, 1)

            def normalise_rows(t, src, mv, rstd, out, step, ready):
                wait(dve, step, at(t, 2, 2))
                for s in range(SUBS):
                    op = nc.vector.tensor_scalar(out[:, s * P:(s + 1) * P], src[:, s * P:(s + 1) * P], mv[:, s, 0:1],
                                                 rstd[:, s:s + 1], ALU.subtract, ALU.mult)
                op.then_inc(ready, 1)

            def row_max(t, u, stats_at=None):
                grid = scores_ps[u % 2][:].rearrange("p (g m) -> p g m", m=WIN)
                wait(dve, scores_done, at(t, UNITS, u + 1))
                if stats_at is not None:
                    wait(dve, stat_step, stats_at)
                nc.vector.tensor_reduce(smax[:, u % 2, :], grid, AX.X, ALU.max).then_inc(max_done, 1)

            def subtract_max(t, u):
                grid = scores_ps[u % 2][:].rearrange("p (g m) -> p g m", m=WIN)
                wait(dve, max_done, at(t, UNITS, u + 1))
                wait(dve, probs_ready, at(t, UNITS, u - 1))
                nc.vector.tensor_tensor(shifted[u % 2][:].rearrange("p (g m) -> p g m", m=WIN), grid,
                                        smax[:, u % 2, :].unsqueeze(2).broadcast_to([P, 16, WIN]),
                                        ALU.subtract).then_inc(shifted_ready, 1)

            def sums(t, u, stats_at=None):
                wait(dve, probs_ready, at(t, UNITS, u + 1))
                if stats_at is not None:
                    wait(dve, stat_step, stats_at)
                nc.vector.tensor_reduce(psums[:, u % 2, :], probs[u % 2][:].rearrange("p (g m) -> p g m", m=WIN),
                                        AX.X, ALU.add).then_inc(sum_done, 1)
                wait(dve, sum_done, at(t, UNITS, u + 1))
                wait(dve, normed, at(t, UNITS, u - 1))
                nc.vector.reciprocal(rinv[:, u % 2, :], psums[:, u % 2, :]).then_inc(rinv_ready, 1)

            def rotate(n, out, b, table):
                wait(dve, bank_written, n + 1)
                nc.vector.scalar_tensor_tensor(
                    out=out[:].rearrange("p (s m) -> p s m", m=WIN),
                    in0=shared_ps[:].rearrange("p (s m) -> p s m", m=WIN), scalar=bias(b),
                    in1=table.unsqueeze(1).broadcast_to([P, SEQS, WIN]), op0=ALU.add, op1=ALU.mult).then_inc(bank_read, 1)

            def gate_first(t, n):
                wait(dve, bank_written, n + 1)
                nc.vector.tensor_tensor(logits[:].rearrange("p s e -> p (s e)"), shared_ps[:, 0:SUBS * ROUTED],
                                        gate_b[:], ALU.add).then_inc(bank_read, 1)
                dve.wait_ge(bank_read, n + 1)
                nc.vector.tensor_reduce(lmax[:], logits[:], AX.X, ALU.max).then_inc(gate_step, 1)
                e_of_j = logits[:].unsqueeze(2).broadcast_to([P, SUBS, ROUTED, ROUTED])
                e_own = logits[:].unsqueeze(3).broadcast_to([P, SUBS, ROUTED, ROUTED])
                nc.vector.tensor_tensor(pairdiff[:], e_of_j, e_own, ALU.subtract).then_inc(gate_step, 1)
                wait(dve, gate_step, at(t, GATE_STEPS, 2))
                nc.vector.tensor_tensor(lshift[:], logits[:], lmax[:].unsqueeze(2).broadcast_to(G),
                                        ALU.subtract).then_inc(gate_step, 1)
                nc.vector.tensor_tensor(beats[:].rearrange("p s e j -> p (s e j)"),
                                        pairdiff[:].rearrange("p s e j -> p (s e j)"), tiebreak,
                                        ALU.is_ge).then_inc(gate_step, 1)
                wait(dve, gate_step, at(t, GATE_STEPS, 4))
                nc.vector.tensor_reduce(rank[:], beats[:], AX.X, ALU.add).then_inc(gate_step, 1)

            def gate_second(t):
                wait(dve, lexp_ready, at(t, 1, 1))
                nc.vector.tensor_reduce(lsum[:], lexp[:], AX.X, ALU.add).then_inc(gate_step, 1)
                wait(dve, gate_step, at(t, GATE_STEPS, 6))
                nc.vector.reciprocal(linv[:], lsum[:]).then_inc(gate_step, 1)
                nc.vector.scalar_tensor_tensor(out=chosen[:], in0=rank[:], scalar=TOPK - 0.5, in1=lexp[:],
                                               op0=ALU.is_lt, op1=ALU.mult).then_inc(gate_step, 1)
                wait(dve, gate_step, at(t, GATE_STEPS, 8))
                nc.vector.tensor_tensor(cw[:], chosen[:], linv[:].unsqueeze(2).broadcast_to(G),
                                        ALU.mult).then_inc(gate_step, 1)
                wait(dve, gate_step, at(t, GATE_STEPS, 9))
                nc.vector.tensor_copy(cw_parts[:, :, 0:ROUTED], cw[:]).then_inc(gate_step, 1)

            def body(t, m0, closing, opening, units=True):
                use, _n = shared_bank_uses(closing, opening)
                b = {k: m0 + v for k, v in use.items()}
                if units:
                    row_max(t, 0)
                    subtract_max(t, 0)
                    row_max(t, 1)
                    subtract_max(t, 1)
                if opening:
                    wait(dve, x_loaded, at(t + 1, 16, 16))
                    row_stats(x_in, stats)
                    if not units:
                        dve.wait_ge(stat_step, ln_count(t, True, opening))
                if units:
                    sums(t, 0, ln_count(t, True, opening) if opening else None)
                if opening:
                    merge_stats(stats, mv1, ln1_done)
                if closing:
                    wait(dve, bank_written, b["proj"] + 1)
                    wait(dve, xres_biased, at(t - 1, 1, 1))
                    nc.vector.tensor_tensor(x2[:], shared_ps[:], x_res[:], ALU.add).then_inc(bank_read, 1)
                    wait(dve, bank_read, b["proj"] + 1)
                    row_stats(x2, stats2, begun=x2_ready)
                    if not units:
                        dve.wait_ge(stat_step, ln_count(t, False, opening))
                if units:
                    row_max(t, 2, ln_count(t, False, opening) if closing else None)
                if closing:
                    merge_stats(stats2, mv2, ln2_done)
                if opening:
                    normalise_rows(t + 1, x_in, mv1, rstd1, xn, rstd1_step, xn_ready)
                if units:
                    subtract_max(t, 2)
                if closing:
                    normalise_rows(t - 1, x2, mv2, rstd2, xn2, rstd2_step, xn2_ready)
                if units:
                    sums(t, 1)
                if closing:
                    gate_first(t - 1, b["gate"])
                if units:
                    row_max(t, 3)
                    subtract_max(t, 3)
                    sums(t, 2)
                if closing:
                    gate_second(t - 1)
                if opening:
                    rotate(b["q"], q_cos, "q", cos)
                    rotate(b["qs"], q_sin, "qs", sin)
                if units:
                    sums(t, 3)
                if opening:
                    rotate(b["k"], k_cos, "k", cos)
                    rotate(b["ks"], k_sin, "ks", sin)

            def ln_count(t, first, opening):
                if isinstance(t, int) and t <= 0:
                    return t + 2
                if not opening:
                    return 2 * TILES - 1 + (t - (TILES - 1))
                return 2 * t + (1 if first else 2)

            dve.wait_ge(weights_in, 16 * SETUP_DMAS)
            nc.vector.tensor_copy(ident_bf[:], ident).then_inc(dve_casts, 1)
            nc.vector.tensor_copy(keep["sel"][:].rearrange("p e n -> p (e n)"), probs[1][0:CW_ROWS, :]).then_inc(dve_casts, 1)
            b2, parts = keep["b2"], keep["b2_parts"]
            nc.vector.tensor_copy(parts[:, 0, :], b2[:]).then_inc(dve_casts, 1)
            dve.wait_ge(dve_casts, 3)
            nc.vector.tensor_tensor(b2[:], b2[:], parts[:, 0, :], ALU.subtract).then_inc(dve_casts, 1)
            dve.wait_ge(dve_casts, 4)
            nc.vector.tensor_copy(parts[:, 1, :], b2[:]).then_inc(dve_casts, 1)
            dve.wait_ge(dve_casts, 5)
            nc.vector.tensor_tensor(parts[:, 2, :], b2[:], parts[:, 1, :], ALU.subtract).then_inc(dve_casts, 1)
            run_iterations(dve, body)

        @block.gpsimd
        def _(pool):
            def inverse_std(t, mv, ve, rstd, eps, done, step):
                wait(pool, done, at(t, 1, 1))
                nc.gpsimd.tensor_tensor(ve[:], mv[:, :, 1], eps[:], ALU.add).then_inc(step, 1)
                wait(pool, step, at(t, 2, 1))
                nc.gpsimd.tensor_tensor(rstd[:], ve[:], half_neg[:], ALU.pow).then_inc(step, 1)

            def normalise(t, u):
                wait(pool, rinv_ready, at(t, UNITS, u + 1))
                grid = probs[u % 2][:].rearrange("p (g m) -> p g m", m=WIN)
                nc.gpsimd.tensor_tensor(grid, grid, rinv[:, u % 2, :].unsqueeze(2).broadcast_to([P, 16, WIN]),
                                        ALU.mult).then_inc(normed, 1)

            def split_cw(t):
                wait(pool, gate_step, at(t, GATE_STEPS, CW_FIRST))
                nc.gpsimd.tensor_tensor(cw_rest[:], cw[:], cw_parts[:, :, 0:ROUTED], ALU.subtract).then_inc(parts_step, 1)
                wait(pool, parts_step, at(t, 2, 1))
                nc.gpsimd.tensor_tensor(cw_parts[:, :, ROUTED:2 * ROUTED], cw_rest[:], zeros[:],
                                        ALU.add).then_inc(parts_step, 1)
                wait(pool, parts_step, at(t, 2, 2))
                nc.gpsimd.tensor_tensor(cw_parts[:, :, 2 * ROUTED:3 * ROUTED], cw_rest[:],
                                        cw_parts[:, :, ROUTED:2 * ROUTED], ALU.subtract).then_inc(cw_ready, 1)

            def split_w_lo(t):
                for j in range(W_PER_TILE):
                    n = t * W_PER_TILE + j
                    wait(pool, w_hi_ready, at(t, W_PER_TILE, j + 1))
                    nc.gpsimd.tensor_tensor(w_block(keep["w_lo"], n), w_stage[:, j, :],
                                            w_block(keep["w_hi"], n).bitcast(F32), ALU.subtract).then_inc(w_lo_ready, 1)

            def body(t, m0, closing, opening, units=True):
                use, _n = shared_bank_uses(closing, opening)
                b = {k: m0 + v for k, v in use.items()}
                if closing:
                    wait(pool, xres_loaded, at(t - 1, 16, 16))
                    nc.gpsimd.tensor_tensor(x_res[:], x_res[:], proj_b[:], ALU.add).then_inc(xres_biased, 1)
                if opening:
                    inverse_std(t + 1, mv1, ve1, rstd1, eps_conv, ln1_done, rstd1_step)
                if units:
                    normalise(t, 0)
                if closing:
                    inverse_std(t - 1, mv2, ve2, rstd2, eps_ffn, ln2_done, rstd2_step)
                if units:
                    normalise(t, 1)
                    normalise(t, 2)
                if closing:
                    split_cw(t - 1)
                if opening:
                    wait(pool, bank_read, b["qs"] + 1)
                    wait(pool, scores_done, at(t + 1, UNITS, 0))
                    nc.gpsimd.tensor_tensor(q_rot[:], q_cos[:], q_sin[:], ALU.add).then_inc(q_ready, 1)
                if units:
                    normalise(t, 3)
                if opening:
                    wait(pool, bank_read, b["ks"] + 1)
                    nc.gpsimd.tensor_tensor(k_rot[:], k_cos[:], k_sin[:], ALU.add).then_inc(k_ready, 1)
                if units:
                    split_w_lo(t)

            nc.gpsimd.memset(half_neg[:], -0.5).then_inc(pool_fills, 1)
            nc.gpsimd.memset(eps_conv[:], EPS_CONV).then_inc(pool_fills, 1)
            nc.gpsimd.memset(eps_ffn[:], EPS_FFN).then_inc(pool_fills, 1)
            nc.gpsimd.memset(zeros[:], 0.0).then_inc(pool_fills, 1)
            nc.gpsimd.memset(v_spread[:], 0.0).then_inc(pool_fills, 1)
            nc.gpsimd.memset(cw_parts[:], 1.0).then_inc(pool_fills, 1)
            pool.wait_ge(pool_fills, POOL_FILLS)
            pool.wait_ge(weights_in, 16 * SETUP_DMAS)
            run_iterations(pool, body)


def experts_phase(nc, d, keep):
    RING, M_RING, H_RING, UP_BANKS = 8, 4, 4, 4
    SH, RO = SHARED * FC, ROUTED * FC
    DVE_SHARE = 3
    DVE_LOWS, POOL_LOWS = EXPERTS, CHUNKS - EXPERTS
    with ExitStack() as ctx:
        def sb(name, shape, dt=F32):
            return ctx.enter_context(nc.sbuf_tensor(name, shape, dt))

        def psum(name, shape):
            return ctx.enter_context(nc.psum_tensor(name, shape, F32))

        def sem(name):
            return ctx.enter_context(nc.semaphore(name))

        up_ps = [psum(f"up_ps{i}", [P, TILE]) for i in range(UP_BANKS)]
        cw_ps = [psum(f"cw_ps{i}", [P, TILE]) for i in range(2)]
        y_ps = psum("y_ps", [P, TILE])
        x_hi, x_lo = sb("x_hi", [P, TILE], F32R), sb("x_lo", [P, TILE], F32R)
        cwT_now = sb("cwT_now", [CW_ROWS, TILE], BF16)
        h = [sb(f"h{i}", [P, TILE]) for i in range(H_RING)]
        m = [sb(f"m{i}", [P, TILE]) for i in range(M_RING)]
        m_hi = [sb(f"m_hi{i}", [P, TILE], F32R) for i in range(RING)]
        m_lo = [sb(f"m_lo{i}", [P, TILE], F32R) for i in range(RING)]
        y_sb = sb("y_sb", [P, TILE])

        x_hi_ready, x_lo_ready, cwT_ready = sem("x_hi_ready"), sem("x_lo_ready"), sem("cwT_ready")
        up_done, cw_spread, down_done = sem("up_done"), sem("cw_spread"), sem("down_done")
        gelu_done, scaled = sem("gelu_done"), sem("scaled")
        hi_shared, hi_routed = sem("hi_shared"), sem("hi_routed")
        lo_by_dve, lo_by_pool = sem("lo_by_dve"), sem("lo_by_pool")
        y_ready, y_stored = sem("y_ready"), sem("y_stored")

        def weights(n, part):
            return keep[part][:, n * P:(n + 1) * P]

        def wait_low_part(eng, t, n):
            tile, n = (t, n) if n >= 0 else (t - 1, n + CHUNKS)
            by_dve = sum(1 for i in range(n + 1) if i % FC == DVE_SHARE)
            if n % FC == DVE_SHARE:
                eng.wait_ge(lo_by_dve, at(tile, DVE_LOWS, by_dve))
            else:
                eng.wait_ge(lo_by_pool, at(tile, POOL_LOWS, n + 1 - by_dve))

        block = ctx.enter_context(nc.Block())

        @block.sync
        def _(sp):
            sp.sem_inc(y_stored, 16)
            with sp.Fori(1, TILES + 1) as t:
                sp.wait_ge(y_ready, at(t, 1, 1))
                sp.dma_start(d["yT"][:, bass.ds((t - 1) * TILE, TILE)], y_sb[:]).then_inc(y_stored, 16)
            sp.wait_ge(y_stored, 16 * (TILES + 1))

        @block.tensor
        def _(pe):
            def three_passes(out, n, hi, lo, start, stop):
                nc.tensor.matmul(out, weights(n, "w_hi"), hi, start=start, stop=False, skip_group_check=True)
                nc.tensor.matmul(out, weights(n, "w_hi"), lo, start=False, stop=False, skip_group_check=True)
                return nc.tensor.matmul(out, weights(n, "w_lo"), hi, start=False, stop=stop, skip_group_check=True)

            def up(t, n):
                pe.wait_ge(gelu_done, at(t, CHUNKS, n - UP_BANKS + 1))
                three_passes(up_ps[n % UP_BANKS][:], n, x_hi[:], x_lo[:], True, True).then_inc(up_done, 1)

            def spread_cw(t, e):
                pe.wait_ge(scaled, at(t, RO, FC * (e - SHARED - 1)))
                nc.tensor.matmul(cw_ps[e % 2][:], keep["sel"][:, e - SHARED, :], cwT_now[:],
                                 start=True, stop=True).then_inc(cw_spread, 1)

            def out_biases(t):
                pe.wait_ge(y_ready, at(t, 1, 0))
                for part in range(3):
                    nc.tensor.matmul(y_ps[:], keep["b2_parts"][:, part, :], cwT_now[:],
                                     start=(part == 0), stop=False, skip_group_check=True)

            def down(t, n):
                wait_low_part(pe, t, n)
                three_passes(y_ps[:], CHUNKS + n, m_hi[n % RING][:], m_lo[n % RING][:], False,
                             n == CHUNKS - 1).then_inc(down_done, 1)

            pe.sem_inc(up_done, CHUNKS)
            pe.sem_inc(cw_spread, ROUTED)
            pe.sem_inc(down_done, CHUNKS)
            with pe.Fori(1, TILES + 1) as t:
                pe.wait_ge(x_lo_ready, at(t, 1, 1))
                for e in range(EXPERTS):
                    if e == 1:
                        pe.wait_ge(cwT_ready, at(t, 1, 1))
                        out_biases(t)
                    if e >= SHARED:
                        spread_cw(t, e)
                    for c in range(FC):
                        up(t, e * FC + c)
                        if e >= 1:
                            down(t, (e - 1) * FC + c)
                for c in range(FC):
                    down(t, (EXPERTS - 1) * FC + c)

        @block.scalar
        def _(act):
            act.sem_inc(gelu_done, CHUNKS)
            act.sem_inc(hi_shared, SH)
            act.sem_inc(x_hi_ready, 1)
            with act.Fori(1, TILES + 1) as t:
                act.wait_ge(up_done, at(t, CHUNKS, 0))
                nc.scalar.copy(x_hi[:], keep["xn2T"][:, bass.ds((t - 1) * TILE, TILE)]).then_inc(x_hi_ready, 1)
                for n in range(CHUNKS):
                    act.wait_ge(up_done, at(t, CHUNKS, n + 1))
                    if n < SH:
                        wait_low_part(act, t, n - M_RING)
                        out = m[n % M_RING]
                    else:
                        act.wait_ge(scaled, at(t, RO, n - SH - H_RING + 1))
                        out = h[n % H_RING]
                    nc.scalar.activation(out[:], up_ps[n % UP_BANKS][:], ACT.Gelu,
                                         bias=keep["bias"][:, BIAS_AT["b1"]][:, n:n + 1]).then_inc(gelu_done, 1)
                    if n < SH:
                        act.wait_ge(gelu_done, at(t, CHUNKS, n + 1))
                        act.wait_ge(down_done, at(t, CHUNKS, n - RING + 1))
                        nc.scalar.copy(m_hi[n % RING][:], m[n % M_RING][:]).then_inc(hi_shared, 1)

        @block.vector
        def _(dve):
            def scale(t, n):
                e = n // FC
                dve.wait_ge(gelu_done, at(t, CHUNKS, n + 1))
                dve.wait_ge(cw_spread, at(t, ROUTED, e - SHARED + 1))
                wait_low_part(dve, t, n - M_RING)
                nc.vector.tensor_tensor(m[n % M_RING][:], cw_ps[e % 2][:], h[n % H_RING][:], ALU.mult).then_inc(scaled, 1)

            def high_part(t, n):
                dve.wait_ge(scaled, at(t, RO, n - SH + 1))
                dve.wait_ge(down_done, at(t, CHUNKS, n - RING + 1))
                nc.vector.tensor_copy(m_hi[n % RING][:], m[n % M_RING][:]).then_inc(hi_routed, 1)

            def low_part(t, n):
                if n < SH:
                    dve.wait_ge(hi_shared, at(t, SH, n + 1))
                else:
                    dve.wait_ge(hi_routed, at(t, RO, n - SH + 1))
                nc.vector.tensor_tensor(m_lo[n % RING][:], m[n % M_RING][:], m_hi[n % RING][:].bitcast(F32),
                                        ALU.subtract).then_inc(lo_by_dve, 1)

            dve.sem_inc(scaled, RO)
            dve.sem_inc(hi_routed, RO)
            dve.sem_inc(lo_by_dve, DVE_LOWS)
            dve.sem_inc(y_ready, 1)
            with dve.Fori(1, TILES + 1) as t:
                for n in range(CHUNKS + 2):
                    if SH <= n < CHUNKS:
                        scale(t, n)
                    if SH <= n - 1 < CHUNKS:
                        high_part(t, n - 1)
                    if n >= 2 and (n - 2) % FC == DVE_SHARE:
                        low_part(t, n - 2)
                dve.wait_ge(down_done, at(t, CHUNKS, CHUNKS))
                dve.wait_ge(y_stored, at(t, 16, 0))
                nc.vector.tensor_tensor(y_sb[:], y_ps[:], keep["x2T"][:, bass.ds((t - 1) * TILE, TILE)],
                                        ALU.add).then_inc(y_ready, 1)

        @block.gpsimd
        def _(pool):
            pool.sem_inc(x_lo_ready, 1)
            pool.sem_inc(cwT_ready, 1)
            pool.sem_inc(lo_by_pool, POOL_LOWS)
            with pool.Fori(1, TILES + 1) as t:
                pool.wait_ge(x_hi_ready, at(t, 1, 1))
                nc.gpsimd.tensor_tensor(x_lo[:], keep["xn2T"][:, bass.ds((t - 1) * TILE, TILE)], x_hi[:].bitcast(F32),
                                        ALU.subtract).then_inc(x_lo_ready, 1)
                pool.wait_ge(cw_spread, at(t, ROUTED, 0))
                nc.gpsimd.tensor_copy(cwT_now[:], keep["cwT"][:, bass.ds((t - 1) * TILE, TILE)]).then_inc(cwT_ready, 1)
                for n in range(CHUNKS):
                    if n % FC == DVE_SHARE:
                        continue
                    if n < SH:
                        pool.wait_ge(hi_shared, at(t, SH, n + 1))
                    else:
                        pool.wait_ge(hi_routed, at(t, RO, n - SH + 1))
                    nc.gpsimd.tensor_tensor(m_lo[n % RING][:], m[n % M_RING][:], m_hi[n % RING][:].bitcast(F32),
                                            ALU.subtract).then_inc(lo_by_pool, 1)


def build(nc, d):
    with ExitStack() as ctx:
        def sb(name, shape, dt=F32):
            return ctx.enter_context(nc.sbuf_tensor(name, shape, dt))

        keep = {
            "const": sb("const", [P, CONST_N]), "bias": sb("bias", [P, BIAS_N]),
            "b2": sb("b2", [CW_ROWS, P]), "b2_parts": sb("b2_parts", [CW_ROWS, 3, P], BF16),
            "sel": sb("sel", [CW_ROWS, ROUTED, P], BF16),
            "w_hi": sb("w_hi", [P, W_COLS], F32R), "w_lo": sb("w_lo", [P, W_COLS], F32R),
            "x2T": sb("x2T", [P, TOKENS]), "xn2T": sb("xn2T", [P, TOKENS]),
            "cwT": sb("cwT", [CW_ROWS, TOKENS], BF16),
        }
        attention_phase(nc, d, keep)
        experts_phase(nc, d, keep)


def constants():
    ident = np.eye(P, dtype=np.float32)
    inv = (1.0 / np.float32(10000.0) ** (np.arange(0, HD // 2, 2, dtype=np.float32) / np.float32(HD // 2))).astype(np.float32)
    rows, cols = np.divmod(np.arange(WIN), 8)
    cos, sin = np.zeros((P, WIN), np.float32), np.zeros((P, WIN), np.float32)
    for ch in range(P):
        c = ch % HD
        pos = (rows if c < HD // 2 else cols).astype(np.float32)
        angle = pos * inv[(c % (HD // 2)) // 2]
        cos[ch] = np.cos(angle)
        sin[ch] = np.sin(angle) * (-1.0 if c % 2 == 0 else 1.0)
    headmask = (np.arange(P)[:, None] % 32 // HD == np.arange(HPR)[None]).astype(np.float32)
    e, j = np.meshgrid(np.arange(ROUTED), np.arange(ROUTED), indexing="ij")
    tiebreak = np.where(j < e, 0.0, MIN_NORMAL).astype(np.float32).reshape(-1)
    tiebreak = np.broadcast_to(np.tile(tiebreak, SUBS), (P, SUBS * ROUTED * ROUTED))
    const = np.concatenate([ident, cos, sin, headmask, tiebreak], axis=1)
    sel = np.zeros((CW_ROWS, ROUTED, P), np.float32)
    for part in range(3):
        for e in range(ROUTED):
            sel[part * ROUTED + e, e] = 1.0
    return np.ascontiguousarray(const), sel.reshape(CW_ROWS, ROUTED * P)


def windows(x):
    x = x.reshape(4, 2, 8, 2, 2, 8, 2, C)
    return x.transpose(0, 1, 4, 3, 6, 2, 5, 7).reshape(TOKENS, C)


def images(y):
    y = y.reshape(4, 2, 2, 2, 2, 8, 8, C)
    return y.transpose(0, 1, 5, 3, 2, 6, 4, 7).reshape(4, 32, 32, C)


def kernel(x, L0_conv_qkv_w, L0_conv_qkv_b, L0_conv_proj_w, L0_conv_proj_b, L0_ffn_gate_w, L0_ffn_gate_b,
           L0_ffn_sw1, L0_ffn_sb1, L0_ffn_sw2, L0_ffn_sb2, L0_ffn_rw1, L0_ffn_rb1, L0_ffn_rw2, L0_ffn_rb2):
    import concourse.bacc as _bacc
    from concourse.bass_utils import run_bass_kernel_spmd as _run

    A = np.asarray
    swap = np.arange(P).reshape(-1, 2)[:, ::-1].reshape(-1)
    qkv_w, qkv_b = A(L0_conv_qkv_w), A(L0_conv_qkv_b)
    q_w, k_w, v_w = qkv_w[0:P], qkv_w[P:2 * P], qkv_w[2 * P:]
    q_b, k_b, v_b = qkv_b[0:P], qkv_b[P:2 * P], qkv_b[2 * P:]
    const, sel = constants()
    w1 = np.concatenate([A(L0_ffn_sw1), A(L0_ffn_rw1)])
    w2 = np.concatenate([A(L0_ffn_sw2), A(L0_ffn_rw2)])
    b1 = np.concatenate([A(L0_ffn_sb1), A(L0_ffn_rb1)])
    up = w1.transpose(2, 0, 1).reshape(P, CHUNKS * P)
    down = w2.reshape(EXPERTS, C, FC, P).transpose(3, 0, 2, 1).reshape(P, CHUNKS * P)
    w12 = np.concatenate([up, down], axis=1).reshape(P, TILES * W_PER_TILE, W_BLOCK).transpose(1, 0, 2)
    b1 = b1.reshape(EXPERTS, FC, P).transpose(2, 0, 1).reshape(P, CHUNKS)
    arrays = {
        "x": windows(A(x)).reshape(TILES, SUBS, P, C).transpose(0, 2, 1, 3).reshape(TILES, P, TILE),
        "wqkv": np.concatenate([q_w.T, q_w[swap].T, k_w.T, k_w[swap].T, v_w.T, A(L0_conv_proj_w).T], axis=1),
        "bias": np.concatenate([q_b[:, None], q_b[swap][:, None], k_b[:, None], k_b[swap][:, None], v_b[:, None], b1],
                               axis=1),
        "const": const, "sel": sel,
        "proj_b": np.tile(A(L0_conv_proj_b), (P, SUBS)),
        "gate_w": A(L0_ffn_gate_w).T,
        "gate_b": np.tile(A(L0_ffn_gate_b), (P, SUBS)),
        "w12": w12,
        "b2": np.concatenate([np.tile(A(L0_ffn_rb2), (3, 1)), A(L0_ffn_sb2)]),
    }
    nc = _bacc.Bacc("TRN2", target_bir_lowering=False, num_devices=1)
    d, ins = {}, {}
    for name, a in arrays.items():
        ins[f"{name}_dram"] = a = np.ascontiguousarray(a)
        d[name] = nc.dram_tensor(f"{name}_dram", a.shape, mybir.dt.from_np(a.dtype), kind="ExternalInput").ap()
    d["yT"] = nc.dram_tensor("out_0_dram", (C, TOKENS), F32, kind="ExternalOutput").ap()
    build(nc, d)
    r = _run(nc, [ins], core_ids=[0])
    return images(r.results[0]["out_0_dram"].T)
```

```python
from contextlib import ExitStack

import numpy as np

import concourse.bass as bass
from concourse import mybir

F32 = mybir.dt.float32
F32R = mybir.dt.float32r
BF16 = mybir.dt.bfloat16
ALU = mybir.AluOpType
ACT = mybir.ActivationFunctionType
AX = mybir.AxisListType

P = 128
C = 128
TOKENS = 4096
TILE = 512
TILES = TOKENS // TILE
SUBS = TILE // P
WIN = 64
SEQS = TILE // WIN
HEADS, HD = 16, 8
SCALE = HD ** -0.5
HPR = 4
UNITS = 4
SHARED, ROUTED, TOPK = 2, 8, 2
EXPERTS = SHARED + ROUTED
FC = 4
CHUNKS = EXPERTS * FC
CW_ROWS = 3 * ROUTED + SHARED
SH, RO = SHARED * FC, ROUTED * FC
EPS_CONV, EPS_FFN = 1e-6, 1e-5
MIN_NORMAL = 1.1754944e-38
W_COLS = 2 * CHUNKS * P
W_BLOCK = TILE
W_BLOCKS = W_COLS // W_BLOCK
W_EVERY = 2

LAG = 6
STEPS = CHUNKS + LAG
CWT = 1
LN1, XNT, Q, QS, K, KS, V = 0, 3, 4, 5, 6, 7, (8, 9)
SCORES = (11, 14, 17, 20)
EXP = {16: (0, 1), 22: (2, 3)}
SUMS = (18, 20, 24, 26)
VALUES = (22, 25, 28, 31)
PROJ, X2T, XN2T, GATE, GATE_EXP, GATE_END = 34, 36, 39, 40, 42, 43

QKV_BLOCKS = 6
CONST_COLS = {"ident": P, "cos": WIN, "sin": WIN, "headmask": HPR, "tiebreak": SUBS * ROUTED * ROUTED}
BIAS_COLS = {"q": 1, "qs": 1, "k": 1, "ks": 1, "v": 1, "b1": CHUNKS}


def offsets(cols):
    at, out = 0, {}
    for name, n in cols.items():
        out[name] = slice(at, at + n)
        at += n
    return out, at


CONST_AT, CONST_N = offsets(CONST_COLS)
BIAS_AT, BIAS_N = offsets(BIAS_COLS)


def at(tile, per_tile, k):
    return tile * per_tile + k


def wait(eng, sem, value):
    if isinstance(value, int) and value <= 0:
        return
    eng.wait_ge(sem, value)


def tile_of(tensor, n):
    if isinstance(n, int):
        return tensor[n]
    return tensor[bass.ds(n, 1), :, :].rearrange("o p n -> p (o n)")


def build(nc, d):
    RING, M_RING, H_RING, UP_BANKS = 8, 4, 4, 2
    DVE_SHARE = 3
    DVE_LOWS, POOL_LOWS = EXPERTS, CHUNKS - EXPERTS
    BANK = 16
    (B_XNT, B_Q, B_QS, B_K, B_KS, B_V0, B_V1, B_PV0, B_PV1, B_PV2, B_PV3, B_PROJ, B_X2T, B_XN2T, B_GATE,
     B_CWT) = range(BANK)
    STAGES = H_RING
    GATE_STEPS, LSHIFT, CW_FIRST = 10, 3, 10
    SETUP_DMAS, POOL_FILLS, DVE_CASTS = 8, 6, 6

    with ExitStack() as ctx:
        def sb(name, shape, dt=F32):
            return ctx.enter_context(nc.sbuf_tensor(name, shape, dt))

        def psum(name, shape):
            return ctx.enter_context(nc.psum_tensor(name, shape, F32))

        def sem(name):
            return ctx.enter_context(nc.semaphore(name))

        scores_ps = psum("scores_ps", [P, 1024])
        probsT_ps = psum("probsT_ps", [P, TILE])
        shared_ps = psum("shared_ps", [P, TILE])
        up_ps = [psum(f"up_ps{i}", [P, TILE]) for i in range(UP_BANKS)]
        cw_ps = psum("cw_ps", [P, TILE])
        y_ps = psum("y_ps", [P, TILE])

        const, biases = sb("const", [P, CONST_N]), sb("biases", [P, BIAS_N])
        b2, b2_parts = sb("b2", [CW_ROWS, P]), sb("b2_parts", [CW_ROWS, 3, P], BF16)
        sel = sb("sel", [CW_ROWS, ROUTED, P], BF16)
        w_hi, w_lo = sb("w_hi", [P, W_COLS], F32R), sb("w_lo", [P, W_COLS], F32R)
        wqkv = sb("wqkv", [P, QKV_BLOCKS * P])
        gate_w = sb("gate_w", [P, ROUTED])
        gate_b = sb("gate_b", [P, SUBS * ROUTED])
        proj_b = sb("proj_b", [P, C])
        half_neg = sb("half_neg", [P, SUBS])
        eps_conv, eps_ffn = sb("eps_conv", [P, SUBS]), sb("eps_ffn", [P, SUBS])
        ident_bf = sb("ident_bf", [P, P], BF16)
        x_in, x_res = sb("x_in", [P, TILE]), sb("x_res", [P, TILE])
        stats, stats2 = sb("stats", [P, SUBS, 6]), sb("stats2", [P, SUBS, 6])
        stats_seen = sb("stats_seen", [P, 1])
        mv1, mv2 = sb("mv1", [P, SUBS, 2]), sb("mv2", [P, SUBS, 2])
        ve1, ve2 = sb("ve1", [P, SUBS]), sb("ve2", [P, SUBS])
        rstd1, rstd2 = sb("rstd1", [P, SUBS]), sb("rstd2", [P, SUBS])
        xn, xnT = sb("xn", [P, TILE]), sb("xnT", [P, TILE])
        q_rot, k_rot, sines = sb("q_rot", [P, TILE]), sb("k_rot", [P, TILE]), sb("sines", [P, TILE])
        k_masked = sb("k_masked", [P, SEQS, HPR, WIN])
        v_spread = sb("v_spread", [P, SEQS * (HEADS // 2) * 32 + 32])
        smax, psums, rinv = (sb(n, [P, UNITS, 16]) for n in ("smax", "psums", "rinv"))
        probs = [sb(f"probs{i}", [P, 1024]) for i in range(UNITS)]
        probsT = [sb(f"probsT{i}", [P, 4, P]) for i in range(2)]
        attnT = sb("attnT", [P, TILE])
        x2 = sb("x2", [P, TILE])
        x2T = sb("x2T", [P, 2 * TILE])
        G = [P, SUBS, ROUTED]
        logits, lshift, lexp = sb("logits", G), sb("lshift", G), sb("lexp", G)
        lmax, lsum, linv = (sb(n, [P, SUBS]) for n in ("lmax", "lsum", "linv"))
        pairdiff = sb("pairdiff", [P, SUBS, ROUTED, ROUTED])
        beats = sb("beats", [P, SUBS, ROUTED, ROUTED])
        rank, chosen, cw, cw_rest = sb("rank", G), sb("chosen", G), sb("cw", G), sb("cw_rest", G)
        zeros = sb("zeros", G)
        cw_parts = sb("cw_parts", [P, SUBS, CW_ROWS], BF16)
        cwT = sb("cwT", [CW_ROWS, TILE], BF16)
        x_hi, x_lo = sb("x_hi", [P, TILE], F32R), sb("x_lo", [P, TILE], F32R)
        h = [sb(f"h{i}", [P, TILE]) for i in range(H_RING)]
        m = [sb(f"m{i}", [P, TILE]) for i in range(M_RING)]
        m_hi = [sb(f"m_hi{i}", [P, TILE], F32R) for i in range(RING)]
        m_lo = [sb(f"m_lo{i}", [P, TILE], F32R) for i in range(RING)]
        y_sb = sb("y_sb", [P, TILE])

        constants_in, pool_fills, dve_casts = sem("constants_in"), sem("pool_fills"), sem("dve_casts")
        w_loaded = [sem(f"w_loaded{j}") for j in range(STAGES)]
        w_hi_ready, w_lo_ready = sem("w_hi_ready"), sem("w_lo_ready")
        x_loaded, xres_loaded = sem("x_loaded"), sem("xres_loaded")
        stat_step = sem("stat_step")
        ln1_done, rstd1_step, xn_ready = sem("ln1_done"), sem("rstd1_step"), sem("xn_ready")
        ln2_done, rstd2_step, xn2_ready = sem("ln2_done"), sem("rstd2_step"), sem("xn2_ready")
        bank_written, bank_read = sem("bank_written"), sem("bank_read")
        q_ready, k_ready, k_masked_ready = sem("q_ready"), sem("k_ready"), sem("k_masked_ready")
        scores_done, max_done, shifted_ready = sem("scores_done"), sem("max_done"), sem("shifted_ready")
        probs_ready, sum_done, rinv_ready = sem("probs_ready"), sem("sum_done"), sem("rinv_ready")
        normed, transposed, probsT_ready = sem("normed"), sem("transposed"), sem("probsT_ready")
        pv_half = sem("pv_half")
        xres_biased, x2_ready = sem("xres_biased"), sem("x2_ready")
        gate_step, lexp_ready, cw_ready = sem("gate_step"), sem("lexp_ready"), sem("cw_ready")
        parts_step = sem("parts_step")
        x_hi_ready, x_lo_ready = sem("x_hi_ready"), sem("x_lo_ready")
        up_done, cw_spread, down_done = sem("up_done"), sem("cw_spread"), sem("down_done")
        gelu_done, scaled = sem("gelu_done"), sem("scaled")
        hi_shared, hi_routed = sem("hi_shared"), sem("hi_routed")
        lo_by_dve, lo_by_pool = sem("lo_by_dve"), sem("lo_by_pool")
        y_ready, y_stored = sem("y_ready"), sem("y_stored")

        ident = const[:, CONST_AT["ident"]]
        cos, sin = const[:, CONST_AT["cos"]], const[:, CONST_AT["sin"]]
        headmask, tiebreak = const[:, CONST_AT["headmask"]], const[:, CONST_AT["tiebreak"]]

        def bias(name):
            return biases[:, BIAS_AT[name]]

        def up_weights(part, n):
            e, c = divmod(n, FC)
            return part[:, (2 * e * FC + c) * P:(2 * e * FC + c + 1) * P]

        def down_weights(part, n):
            e, c = divmod(n, FC)
            return part[:, ((2 * e + 1) * FC + c) * P:((2 * e + 1) * FC + c + 1) * P]

        def x2T_of(t):
            half = (t % 2) * TILE
            return x2T[:, half:half + TILE] if isinstance(t, int) else x2T[:, bass.ds(half, TILE)]

        def wait_low_part(eng, t, n):
            tile, n = (t, n) if n >= 0 else (t - 1, n + CHUNKS)
            by_dve = sum(1 for i in range(n + 1) if i % FC == DVE_SHARE)
            if n % FC == DVE_SHARE:
                eng.wait_ge(lo_by_dve, at(tile, DVE_LOWS, by_dve))
            else:
                eng.wait_ge(lo_by_pool, at(tile, POOL_LOWS, n + 1 - by_dve))

        def run_iterations(eng, body):
            body(0, False, True)
            with eng.Fori(1, TILES) as t:
                body(t, True, True)
            body(TILES, True, False)

        block = ctx.enter_context(nc.Block())

        @block.sync
        def _(sp):
            sp.dma_start(x_in[:], d["x"][0]).then_inc(x_loaded, 16)
            sp.dma_start(const[:], d["const"]).then_inc(constants_in, 16)
            sp.dma_start(wqkv[:], d["wqkv"]).then_inc(constants_in, 16)
            sp.dma_start(biases[:], d["bias"]).then_inc(constants_in, 16)
            sp.dma_start(gate_w[:], d["gate_w"]).then_inc(constants_in, 16)
            sp.dma_start(gate_b[:], d["gate_b"]).then_inc(constants_in, 16)
            sp.dma_start(proj_b[:], d["proj_b"]).then_inc(constants_in, 16)
            sp.dma_start(b2[:], d["b2"]).then_inc(constants_in, 16)
            sp.dma_start(probs[3][0:CW_ROWS, :], d["sel"]).then_inc(constants_in, 16)
            sp.dma_start(x_res[:], d["x"][0]).then_inc(xres_loaded, 16)
            for n in range(W_BLOCKS):
                wait(sp, w_lo_ready, n - STAGES + 1)
                sp.dma_start(h[n % STAGES][:], d["w12"][n]).then_inc(w_loaded[n % STAGES], 16)
            sp.sem_inc(y_stored, 16)

            def body(t, experts, attend):
                if attend:
                    wait(sp, xn_ready, at(t, 1, 1))
                    sp.dma_start(x_in[:], tile_of(d["x"], (t + 1) % TILES)).then_inc(x_loaded, 16)
                    wait(sp, x2_ready, at(t, 1, 1))
                    sp.dma_start(x_res[:], tile_of(d["x"], (t + 1) % TILES)).then_inc(xres_loaded, 16)
                if experts:
                    sp.wait_ge(y_ready, at(t, 1, 1))
                    cols = slice((t - 1) * TILE, t * TILE) if isinstance(t, int) else bass.ds((t - 1) * TILE, TILE)
                    sp.dma_start(d["yT"][:, cols], y_sb[:]).then_inc(y_stored, 16)

            run_iterations(sp, body)
            sp.wait_ge(y_stored, 16 * (TILES + 1))

        @block.tensor
        def _(pe):
            def use_bank(t, use):
                wait(pe, bank_read, at(t, BANK, use))

            def transposes(t, use, src):
                use_bank(t, use)
                for s in range(SUBS):
                    mm = nc.tensor.transpose(shared_ps[:, s * P:(s + 1) * P], src[:, s * P:(s + 1) * P], ident)
                mm.then_inc(bank_written, 1)

            def project(t, use, b):
                use_bank(t, use)
                nc.tensor.matmul(shared_ps[:], wqkv[:, b * P:(b + 1) * P], xnT[:],
                                 start=True, stop=True).then_inc(bank_written, 1)

            def project_v(t, quad):
                use_bank(t, B_V0 + quad)
                for s in range(4):
                    seq = quad * 4 + s
                    for h2 in range(2):
                        mm = nc.tensor.matmul(shared_ps[64 * h2:64 * h2 + 64, s * P:(s + 1) * P],
                                              xnT[:, seq * WIN:(seq + 1) * WIN],
                                              wqkv[:, 4 * P:5 * P], start=True, stop=True)
                mm.then_inc(bank_written, 1)

            def scores(t, u):
                quad, half = divmod(u, 2)
                if u == 0:
                    wait(pe, q_ready, at(t, 1, 1))
                    wait(pe, k_masked_ready, at(t, 1, 1))
                wait(pe, shifted_ready, at(t, UNITS, u))
                for pair in range(2):
                    for i in range(2):
                        for s in range(2):
                            seq, rg = quad * 4 + pair * 2 + s, 2 * half + i
                            rows = slice(32 * rg, 32 * rg + 32)
                            c0 = i * 512 + pair * 256
                            mm = nc.tensor.matmul(
                                scores_ps[64 * s:64 * s + 64, c0:c0 + 256], q_rot[rows, seq * WIN:(seq + 1) * WIN],
                                k_masked[rows, seq, :, :].rearrange("p h m -> p (h m)"), start=True, stop=True)
                mm.then_inc(scores_done, 1)

            def probs_transposes(t, u, pair):
                wait(pe, normed, at(t, UNITS, u + 1))
                wait(pe, probsT_ready, at(t, 2 * UNITS, 2 * u + pair))
                for b in range(4):
                    i, h2 = divmod(b, 2)
                    c0 = i * 512 + pair * 256 + h2 * P
                    mm = nc.tensor.transpose(probsT_ps[:, b * P:(b + 1) * P], probs[u][:, c0:c0 + P], ident)
                mm.then_inc(transposed, 1)

            def values(t, u, pair):
                quad, half = divmod(u, 2)
                if pair == 0:
                    use_bank(t, B_PV0 + u)
                wait(pe, probsT_ready, at(t, 2 * UNITS, 2 * u + pair + 1))
                for s in range(2):
                    for h2 in range(2):
                        for i in range(2):
                            rg, seq = 2 * half + i, quad * 4 + pair * 2 + s
                            c0 = 16 + (seq * (HEADS // 2) + 2 * rg + h2) * 32 - 16 * h2
                            col = (pair * 2 + s) * WIN
                            mm = nc.tensor.matmul(shared_ps[32 * rg:32 * rg + 32, col:col + WIN],
                                                  v_spread[:, c0:c0 + 32],
                                                  probsT[pair][:, 2 * i + h2, s * WIN:(s + 1) * WIN],
                                                  start=(h2 == 0), stop=(h2 == 1), skip_group_check=True)
                mm.then_inc(pv_half if pair == 0 else bank_written, 1)

            def out_projection(t):
                use_bank(t, B_PROJ)
                for s in range(SUBS):
                    mm = nc.tensor.matmul(shared_ps[:, s * P:(s + 1) * P], attnT[:, s * P:(s + 1) * P],
                                          wqkv[:, 5 * P:6 * P], start=True, stop=True)
                mm.then_inc(bank_written, 1)

            def gate(t):
                use_bank(t, B_GATE)
                for s in range(SUBS):
                    mm = nc.tensor.matmul(shared_ps[:, s * ROUTED:(s + 1) * ROUTED], xnT[:, s * P:(s + 1) * P],
                                          gate_w[:], start=True, stop=True)
                mm.then_inc(bank_written, 1)

            def combine_weights(t):
                wait(pe, cw_ready, at(t, 1, 1))
                use_bank(t, B_CWT)
                for s in range(SUBS):
                    mm = nc.tensor.transpose(shared_ps[:].bitcast(BF16)[0:CW_ROWS, s * P:(s + 1) * P],
                                             cw_parts[:, s, :], ident_bf[:])
                mm.then_inc(bank_written, 1)

            def attention(t, n):
                if n == XNT:
                    wait(pe, xn_ready, at(t, 1, 1))
                    transposes(t, B_XNT, xn)
                for b, step in enumerate((Q, QS, K, KS)):
                    if n == step:
                        project(t, B_Q + b, b)
                for quad in range(2):
                    if n == V[quad]:
                        project_v(t, quad)
                for u in range(UNITS):
                    if n == SCORES[u]:
                        scores(t, u)
                    for pair in range(2):
                        if n == VALUES[u] + pair:
                            probs_transposes(t, u, pair)
                        if n == VALUES[u] + pair + 1:
                            values(t, u, pair)
                if n == PROJ:
                    out_projection(t)
                if n == X2T:
                    wait(pe, x2_ready, at(t, 1, 1))
                    transposes(t, B_X2T, x2)
                if n == XN2T:
                    wait(pe, xn2_ready, at(t, 1, 1))
                    transposes(t, B_XN2T, xn)
                if n == GATE:
                    gate(t)

            def three_passes(out, weights, n, hi, lo, start, stop):
                nc.tensor.matmul(out, weights(w_hi, n), hi, start=start, stop=False, skip_group_check=True)
                nc.tensor.matmul(out, weights(w_hi, n), lo, start=False, stop=False, skip_group_check=True)
                return nc.tensor.matmul(out, weights(w_lo, n), hi, start=False, stop=stop, skip_group_check=True)

            def up(t, n):
                pe.wait_ge(gelu_done, at(t, CHUNKS, n - UP_BANKS + 1))
                three_passes(up_ps[n % UP_BANKS][:], up_weights, n, x_hi[:], x_lo[:], True, True).then_inc(up_done, 1)

            def spread_cw(t, e):
                pe.wait_ge(scaled, at(t, RO, FC * (e - SHARED)))
                nc.tensor.matmul(cw_ps[:], sel[:, e - SHARED, :], cwT[:], start=True, stop=True).then_inc(cw_spread, 1)

            def out_biases(t):
                pe.wait_ge(y_ready, at(t, 1, 0))
                for part in range(3):
                    nc.tensor.matmul(y_ps[:], b2_parts[:, part, :], cwT[:],
                                     start=(part == 0), stop=False, skip_group_check=True)

            def down(t, n):
                wait_low_part(pe, t, n)
                three_passes(y_ps[:], down_weights, n, m_hi[n % RING][:], m_lo[n % RING][:], False,
                             n == CHUNKS - 1).then_inc(down_done, 1)

            def body(t, experts, attend):
                if experts:
                    pe.wait_ge(x_lo_ready, at(t, 1, 0))
                for n in range(STEPS):
                    if experts:
                        if n < CHUNKS:
                            up(t, n)
                        if n == CWT:
                            combine_weights(t - 1)
                        if n == LAG:
                            pe.wait_ge(bank_read, at(t, BANK, 0))
                            out_biases(t)
                        if n >= LAG:
                            down(t, n - LAG)
                        if SH <= n < CHUNKS and n % FC == 0:
                            spread_cw(t, n // FC)
                    if attend:
                        attention(t, n)

            pe.sem_inc(up_done, CHUNKS)
            pe.sem_inc(cw_spread, ROUTED)
            pe.sem_inc(down_done, CHUNKS)
            pe.wait_ge(constants_in, 16 * SETUP_DMAS)
            pe.wait_ge(pool_fills, POOL_FILLS)
            pe.wait_ge(dve_casts, DVE_CASTS)
            body(0, False, True)
            pe.wait_ge(w_lo_ready, W_BLOCKS)
            with pe.Fori(1, TILES) as t:
                body(t, True, True)
            body(TILES, True, False)

        @block.scalar
        def _(act):
            def from_bank(t, use, out, inp):
                wait(act, bank_written, at(t, BANK, use + 1))
                nc.scalar.copy(out, inp).then_inc(bank_read, 1)

            def exp(t, u):
                wait(act, shifted_ready, at(t, UNITS, u + 1))
                nc.scalar.activation(probs[u][:], probs[u][:], ACT.Exp, scale=SCALE).then_inc(probs_ready, 1)

            def copy_probsT(t, u, pair):
                wait(act, transposed, at(t, 2 * UNITS, 2 * u + pair + 1))
                if pair == 0:
                    wait(act, pv_half, at(t, UNITS, u))
                elif u > 0:
                    wait(act, bank_written, at(t, BANK, B_PV0 + u))
                nc.scalar.copy(probsT[pair][:].rearrange("p b n -> p (b n)"), probsT_ps[:]).then_inc(probsT_ready, 1)

            def copy_attn(t, u):
                quad, half = divmod(u, 2)
                rows = slice(64 * half, 64 * half + 64)
                wait(act, bank_written, at(t, BANK, B_PV0 + u + 1))
                nc.scalar.activation(attnT[rows, quad * 256:quad * 256 + 256], shared_ps[rows, 0:256], ACT.Identity,
                                     bias=bias("v")[rows, :]).then_inc(bank_read, 1)

            def mask_k(t, h):
                if h == 0:
                    wait(act, k_ready, at(t, 1, 1))
                    wait(act, scores_done, at(t, UNITS, 0))
                op = nc.scalar.mul(k_masked[:, :, h, :], k_rot[:].rearrange("p (s m) -> p s m", s=SEQS),
                                   headmask[:, h:h + 1])
                if h == HPR - 1:
                    op.then_inc(k_masked_ready, 1)

            def spread_v(t, quad):
                wait(act, bank_written, at(t, BANK, B_V0 + quad + 1))
                for h2 in range(2):
                    rows = slice(64 * h2, 64 * h2 + 64)
                    groups = 4 * HEADS // 2
                    dst = v_spread[rows, 16 + quad * groups * 32:16 + (quad + 1) * groups * 32].rearrange(
                        "p (g w) -> p g w", w=32)[:, :, h2 * HD:(h2 + 1) * HD]
                    src = shared_ps[rows, :].rearrange("p (g w) -> p g w", w=16)[:, :, h2 * HD:(h2 + 1) * HD]
                    op = nc.scalar.copy(dst, src)
                op.then_inc(bank_read, 1)

            def attention(t, n):
                if n == XNT:
                    from_bank(t, B_XNT, xnT[:], shared_ps[:])
                if V[0] <= n < V[0] + 2:
                    spread_v(t, n - V[0])
                    mask_k(t, 2 * (n - V[0]))
                    mask_k(t, 2 * (n - V[0]) + 1)
                for u in EXP.get(n, ()):
                    exp(t, u)
                for u in range(UNITS):
                    for pair in range(2):
                        if n == VALUES[u] + pair:
                            copy_probsT(t, u, pair)
                    if n == VALUES[u] + 2:
                        copy_attn(t, u)
                if n == X2T:
                    from_bank(t, B_X2T, x2T_of(t), shared_ps[:])
                if n == XN2T:
                    from_bank(t, B_XN2T, xnT[:], shared_ps[:])
                if n == GATE_EXP:
                    wait(act, gate_step, at(t, GATE_STEPS, LSHIFT))
                    nc.scalar.activation(lexp[:], lshift[:], ACT.Exp).then_inc(lexp_ready, 1)

            def gelu(t, n):
                act.wait_ge(up_done, at(t, CHUNKS, n + 1))
                if n < SH:
                    wait_low_part(act, t, n - M_RING)
                    out = m[n % M_RING]
                else:
                    act.wait_ge(scaled, at(t, RO, n - SH - H_RING + 1))
                    out = h[n % H_RING]
                nc.scalar.activation(out[:], up_ps[n % UP_BANKS][:], ACT.Gelu,
                                     bias=bias("b1")[:, n:n + 1]).then_inc(gelu_done, 1)

            def high_part(t, n):
                act.wait_ge(gelu_done, at(t, CHUNKS, n + 1))
                act.wait_ge(down_done, at(t, CHUNKS, n - RING + 1))
                nc.scalar.copy(m_hi[n % RING][:], m[n % M_RING][:]).then_inc(hi_shared, 1)

            def weights_high(n):
                act.wait_ge(w_loaded[n % STAGES], 16 * (n // STAGES + 1))
                nc.scalar.copy(w_hi[:, n * W_BLOCK:(n + 1) * W_BLOCK], h[n % STAGES][:]).then_inc(w_hi_ready, 1)

            def body(t, experts, attend):
                for n in range(STEPS):
                    if experts:
                        if n < CHUNKS:
                            gelu(t, n)
                        if n < SH:
                            high_part(t, n)
                        if n == CWT:
                            wait(act, bank_written, at(t - 1, BANK, B_CWT + 1))
                            act.wait_ge(cw_spread, at(t, ROUTED, 0))
                            nc.scalar.copy(cwT[:], shared_ps[:].bitcast(BF16)[0:CW_ROWS, 0:TILE])\
                                .then_inc(bank_read, 1)
                    if attend:
                        attention(t, n)
                    if attend and n == CHUNKS:
                        if experts:
                            act.wait_ge(up_done, at(t, CHUNKS, CHUNKS))
                        act.wait_ge(bank_read, at(t, BANK, B_XN2T + 1))
                        nc.scalar.copy(x_hi[:], xnT[:]).then_inc(x_hi_ready, 1)
                    if not experts and n % W_EVERY == 0 and n // W_EVERY < W_BLOCKS:
                        weights_high(n // W_EVERY)

            act.sem_inc(gelu_done, CHUNKS)
            act.sem_inc(hi_shared, SH)
            act.wait_ge(constants_in, 16 * SETUP_DMAS)
            act.wait_ge(pool_fills, POOL_FILLS)
            body(0, False, True)
            with act.Fori(1, TILES) as t:
                body(t, True, True)
            body(TILES, True, False)

        @block.vector
        def _(dve):
            def row_stats(src, raw, begun=None):
                for s in range(SUBS):
                    op = nc.vector.bn_stats(raw[:, s, :], src[:, s * P:(s + 1) * P])
                    if s == 0 and begun is not None:
                        op.then_inc(begun, 1)
                op.then_inc(stat_step, 1)

            def merge_stats(t, which, raw, mv, done):
                wait(dve, stat_step, at(t, 2, which + 1))
                nc.vector.tensor_copy(stats_seen[:], raw[:, 0, 0:1])
                for s in range(SUBS):
                    op = nc.vector.bn_aggr(mv[:, s, :], raw[:, s, :])
                op.then_inc(done, 1)

            def normalise_rows(t, src, mv, rstd, out, step, ready):
                wait(dve, step, at(t, 2, 2))
                for s in range(SUBS):
                    op = nc.vector.tensor_scalar(out[:, s * P:(s + 1) * P], src[:, s * P:(s + 1) * P], mv[:, s, 0:1],
                                                 rstd[:, s:s + 1], ALU.subtract, ALU.mult)
                op.then_inc(ready, 1)

            def rotate(t, use, out, b, table):
                wait(dve, bank_written, at(t, BANK, use + 1))
                nc.vector.scalar_tensor_tensor(
                    out=out[:].rearrange("p (s m) -> p s m", m=WIN),
                    in0=shared_ps[:].rearrange("p (s m) -> p s m", m=WIN), scalar=bias(b),
                    in1=table.unsqueeze(1).broadcast_to([P, SEQS, WIN]), op0=ALU.add, op1=ALU.mult).then_inc(bank_read, 1)

            def shift(t, u):
                grid = scores_ps[:].rearrange("p (g m) -> p g m", m=WIN)
                wait(dve, scores_done, at(t, UNITS, u + 1))
                nc.vector.tensor_reduce(smax[:, u, :], grid, AX.X, ALU.max).then_inc(max_done, 1)
                wait(dve, max_done, at(t, UNITS, u + 1))
                wait(dve, transposed, at(t - 1, 2 * UNITS, 2 * u + 2))
                nc.vector.tensor_tensor(probs[u][:].rearrange("p (g m) -> p g m", m=WIN), grid,
                                        smax[:, u, :].unsqueeze(2).broadcast_to([P, 16, WIN]),
                                        ALU.subtract).then_inc(shifted_ready, 1)

            def sums(t, u):
                wait(dve, probs_ready, at(t, UNITS, u + 1))
                nc.vector.tensor_reduce(psums[:, u, :], probs[u][:].rearrange("p (g m) -> p g m", m=WIN),
                                        AX.X, ALU.add).then_inc(sum_done, 1)
                wait(dve, sum_done, at(t, UNITS, u + 1))
                nc.vector.reciprocal(rinv[:, u, :], psums[:, u, :]).then_inc(rinv_ready, 1)

            def residual(t):
                wait(dve, bank_written, at(t, BANK, B_PROJ + 1))
                wait(dve, xres_biased, at(t, 1, 1))
                nc.vector.tensor_tensor(x2[:], shared_ps[:], x_res[:], ALU.add).then_inc(bank_read, 1)
                wait(dve, bank_read, at(t, BANK, B_PROJ + 1))
                row_stats(x2, stats2, begun=x2_ready)

            def gate_first(t):
                wait(dve, bank_written, at(t, BANK, B_GATE + 1))
                nc.vector.tensor_tensor(logits[:].rearrange("p s e -> p (s e)"), shared_ps[:, 0:SUBS * ROUTED],
                                        gate_b[:], ALU.add).then_inc(bank_read, 1)
                wait(dve, bank_read, at(t, BANK, B_GATE + 1))
                nc.vector.tensor_reduce(lmax[:], logits[:], AX.X, ALU.max).then_inc(gate_step, 1)
                e_of_j = logits[:].unsqueeze(2).broadcast_to([P, SUBS, ROUTED, ROUTED])
                e_own = logits[:].unsqueeze(3).broadcast_to([P, SUBS, ROUTED, ROUTED])
                nc.vector.tensor_tensor(pairdiff[:], e_of_j, e_own, ALU.subtract).then_inc(gate_step, 1)
                wait(dve, gate_step, at(t, GATE_STEPS, 2))
                nc.vector.tensor_tensor(lshift[:], logits[:], lmax[:].unsqueeze(2).broadcast_to(G),
                                        ALU.subtract).then_inc(gate_step, 1)
                nc.vector.tensor_tensor(beats[:].rearrange("p s e j -> p (s e j)"),
                                        pairdiff[:].rearrange("p s e j -> p (s e j)"), tiebreak,
                                        ALU.is_ge).then_inc(gate_step, 1)
                wait(dve, gate_step, at(t, GATE_STEPS, 4))
                nc.vector.tensor_reduce(rank[:], beats[:], AX.X, ALU.add).then_inc(gate_step, 1)

            def gate_second(t):
                wait(dve, lexp_ready, at(t, 1, 1))
                nc.vector.tensor_reduce(lsum[:], lexp[:], AX.X, ALU.add).then_inc(gate_step, 1)
                wait(dve, gate_step, at(t, GATE_STEPS, 6))
                nc.vector.reciprocal(linv[:], lsum[:]).then_inc(gate_step, 1)
                nc.vector.scalar_tensor_tensor(out=chosen[:], in0=rank[:], scalar=TOPK - 0.5, in1=lexp[:],
                                               op0=ALU.is_lt, op1=ALU.mult).then_inc(gate_step, 1)
                wait(dve, gate_step, at(t, GATE_STEPS, 8))
                nc.vector.tensor_tensor(cw[:], chosen[:], linv[:].unsqueeze(2).broadcast_to(G),
                                        ALU.mult).then_inc(gate_step, 1)
                wait(dve, gate_step, at(t, GATE_STEPS, 9))
                nc.vector.tensor_copy(cw_parts[:, :, 0:ROUTED], cw[:]).then_inc(gate_step, 1)

            def attention(t, n):
                if n == LN1:
                    wait(dve, x_loaded, at(t, 16, 16))
                    row_stats(x_in, stats)
                    merge_stats(t, 0, stats, mv1, ln1_done)
                if n == XNT - 1:
                    normalise_rows(t, x_in, mv1, rstd1, xn, rstd1_step, xn_ready)
                for step, use, out, b, table in ((Q, B_Q, q_rot, "q", cos), (QS, B_QS, sines, "qs", sin),
                                                 (K, B_K, k_rot, "k", cos), (KS, B_KS, sines, "ks", sin)):
                    if n == step:
                        if step == KS:
                            wait(dve, q_ready, at(t, 1, 1))
                        rotate(t, use, out, b, table)
                for u in range(UNITS):
                    if n == SCORES[u]:
                        shift(t, u)
                    if n == SUMS[u]:
                        sums(t, u)
                if n == PROJ:
                    residual(t)
                    merge_stats(t, 1, stats2, mv2, ln2_done)
                if n == XN2T - 1:
                    normalise_rows(t, x2, mv2, rstd2, xn, rstd2_step, xn2_ready)
                if n == GATE:
                    gate_first(t)
                if n == GATE_END:
                    gate_second(t)

            def scale(t, n):
                dve.wait_ge(gelu_done, at(t, CHUNKS, n + 1))
                dve.wait_ge(cw_spread, at(t, ROUTED, n // FC - SHARED + 1))
                wait_low_part(dve, t, n - M_RING)
                nc.vector.tensor_tensor(m[n % M_RING][:], cw_ps[:], h[n % H_RING][:], ALU.mult).then_inc(scaled, 1)

            def high_part(t, n):
                dve.wait_ge(scaled, at(t, RO, n - SH + 1))
                dve.wait_ge(down_done, at(t, CHUNKS, n - RING + 1))
                nc.vector.tensor_copy(m_hi[n % RING][:], m[n % M_RING][:]).then_inc(hi_routed, 1)

            def low_part(t, n):
                if n < SH:
                    dve.wait_ge(hi_shared, at(t, SH, n + 1))
                else:
                    dve.wait_ge(hi_routed, at(t, RO, n - SH + 1))
                nc.vector.tensor_tensor(m_lo[n % RING][:], m[n % M_RING][:], m_hi[n % RING][:].bitcast(F32),
                                        ALU.subtract).then_inc(lo_by_dve, 1)

            def body(t, experts, attend):
                for n in range(STEPS):
                    if experts:
                        if SH <= n - 1 < CHUNKS:
                            scale(t, n - 1)
                        if SH <= n - 2 < CHUNKS:
                            high_part(t, n - 2)
                        if 0 <= n - 3 < CHUNKS and (n - 3) % FC == DVE_SHARE:
                            low_part(t, n - 3)
                    if attend:
                        attention(t, n)
                if experts:
                    dve.wait_ge(down_done, at(t, CHUNKS, CHUNKS))
                    dve.wait_ge(y_stored, at(t, 16, 0))
                    nc.vector.tensor_tensor(y_sb[:], y_ps[:], x2T_of(t - 1), ALU.add).then_inc(y_ready, 1)

            dve.wait_ge(constants_in, 16 * SETUP_DMAS)
            nc.vector.tensor_copy(ident_bf[:], ident).then_inc(dve_casts, 1)
            nc.vector.tensor_copy(sel[:].rearrange("p e n -> p (e n)"), probs[3][0:CW_ROWS, :]).then_inc(dve_casts, 1)
            nc.vector.tensor_copy(b2_parts[:, 0, :], b2[:]).then_inc(dve_casts, 1)
            dve.wait_ge(dve_casts, 3)
            nc.vector.tensor_tensor(b2[:], b2[:], b2_parts[:, 0, :], ALU.subtract).then_inc(dve_casts, 1)
            dve.wait_ge(dve_casts, 4)
            nc.vector.tensor_copy(b2_parts[:, 1, :], b2[:]).then_inc(dve_casts, 1)
            dve.wait_ge(dve_casts, 5)
            nc.vector.tensor_tensor(b2_parts[:, 2, :], b2[:], b2_parts[:, 1, :], ALU.subtract).then_inc(dve_casts, 1)
            dve.sem_inc(scaled, RO)
            dve.sem_inc(hi_routed, RO)
            dve.sem_inc(lo_by_dve, DVE_LOWS)
            dve.sem_inc(y_ready, 1)
            run_iterations(dve, body)

        @block.gpsimd
        def _(pool):
            def inverse_std(t, mv, ve, rstd, eps, done, step):
                wait(pool, done, at(t, 1, 1))
                nc.gpsimd.tensor_tensor(ve[:], mv[:, :, 1], eps[:], ALU.add).then_inc(step, 1)
                wait(pool, step, at(t, 2, 1))
                nc.gpsimd.tensor_tensor(rstd[:], ve[:], half_neg[:], ALU.pow).then_inc(step, 1)

            def normalise(t, u):
                wait(pool, rinv_ready, at(t, UNITS, u + 1))
                grid = probs[u][:].rearrange("p (g m) -> p g m", m=WIN)
                nc.gpsimd.tensor_tensor(grid, grid, rinv[:, u, :].unsqueeze(2).broadcast_to([P, 16, WIN]),
                                        ALU.mult).then_inc(normed, 1)

            def split_cw(t):
                wait(pool, gate_step, at(t, GATE_STEPS, CW_FIRST))
                nc.gpsimd.tensor_tensor(cw_rest[:], cw[:], cw_parts[:, :, 0:ROUTED], ALU.subtract).then_inc(parts_step, 1)
                wait(pool, parts_step, at(t, 2, 1))
                nc.gpsimd.tensor_tensor(cw_parts[:, :, ROUTED:2 * ROUTED], cw_rest[:], zeros[:],
                                        ALU.add).then_inc(parts_step, 1)
                wait(pool, parts_step, at(t, 2, 2))
                nc.gpsimd.tensor_tensor(cw_parts[:, :, 2 * ROUTED:3 * ROUTED], cw_rest[:],
                                        cw_parts[:, :, ROUTED:2 * ROUTED], ALU.subtract).then_inc(cw_ready, 1)

            def attention(t, n):
                if n == LN1 + 1:
                    inverse_std(t, mv1, ve1, rstd1, eps_conv, ln1_done, rstd1_step)
                if n == XNT:
                    wait(pool, xres_loaded, at(t, 16, 16))
                    rows = x_res[:].rearrange("p (s c) -> p s c", s=SUBS)
                    nc.gpsimd.tensor_tensor(rows, rows, proj_b[:].unsqueeze(1).broadcast_to([P, SUBS, C]), ALU.add).then_inc(xres_biased, 1)
                if n == QS:
                    wait(pool, bank_read, at(t, BANK, B_QS + 1))
                    nc.gpsimd.tensor_tensor(q_rot[:], q_rot[:], sines[:], ALU.add).then_inc(q_ready, 1)
                if n == KS:
                    wait(pool, bank_read, at(t, BANK, B_KS + 1))
                    nc.gpsimd.tensor_tensor(k_rot[:], k_rot[:], sines[:], ALU.add).then_inc(k_ready, 1)
                for u in range(UNITS):
                    if n == SUMS[u]:
                        normalise(t, u)
                if n == PROJ:
                    inverse_std(t, mv2, ve2, rstd2, eps_ffn, ln2_done, rstd2_step)
                if n == CHUNKS + 1:
                    wait(pool, x_hi_ready, at(t, 1, 1))
                    nc.gpsimd.tensor_tensor(x_lo[:], xnT[:], x_hi[:].bitcast(F32), ALU.subtract).then_inc(x_lo_ready, 1)
                if n == GATE_END:
                    split_cw(t)

            def low_part(t, n):
                if n < SH:
                    pool.wait_ge(hi_shared, at(t, SH, n + 1))
                else:
                    pool.wait_ge(hi_routed, at(t, RO, n - SH + 1))
                nc.gpsimd.tensor_tensor(m_lo[n % RING][:], m[n % M_RING][:], m_hi[n % RING][:].bitcast(F32),
                                        ALU.subtract).then_inc(lo_by_pool, 1)

            def weights_low(n):
                pool.wait_ge(w_hi_ready, n + 1)
                cols = slice(n * W_BLOCK, (n + 1) * W_BLOCK)
                nc.gpsimd.tensor_tensor(w_lo[:, cols], h[n % STAGES][:], w_hi[:, cols].bitcast(F32),
                                        ALU.subtract).then_inc(w_lo_ready, 1)

            def body(t, experts, attend):
                for n in range(STEPS):
                    if experts and 0 <= n - 3 < CHUNKS and (n - 3) % FC != DVE_SHARE:
                        low_part(t, n - 3)
                    if attend:
                        attention(t, n)
                    if not experts and n % W_EVERY == 0 and n // W_EVERY < W_BLOCKS:
                        weights_low(n // W_EVERY)

            nc.gpsimd.memset(half_neg[:], -0.5).then_inc(pool_fills, 1)
            nc.gpsimd.memset(eps_conv[:], EPS_CONV).then_inc(pool_fills, 1)
            nc.gpsimd.memset(eps_ffn[:], EPS_FFN).then_inc(pool_fills, 1)
            nc.gpsimd.memset(zeros[:], 0.0).then_inc(pool_fills, 1)
            nc.gpsimd.memset(v_spread[:], 0.0).then_inc(pool_fills, 1)
            nc.gpsimd.memset(cw_parts[:], 1.0).then_inc(pool_fills, 1)
            pool.wait_ge(pool_fills, POOL_FILLS)
            pool.wait_ge(constants_in, 16 * SETUP_DMAS)
            pool.sem_inc(lo_by_pool, POOL_LOWS)
            run_iterations(pool, body)


def constants():
    ident = np.eye(P, dtype=np.float32)
    inv = (1.0 / np.float32(10000.0) ** (np.arange(0, HD // 2, 2, dtype=np.float32) / np.float32(HD // 2))).astype(np.float32)
    rows, cols = np.divmod(np.arange(WIN), 8)
    cos, sin = np.zeros((P, WIN), np.float32), np.zeros((P, WIN), np.float32)
    for ch in range(P):
        c = ch % HD
        pos = (rows if c < HD // 2 else cols).astype(np.float32)
        angle = pos * inv[(c % (HD // 2)) // 2]
        cos[ch] = np.cos(angle)
        sin[ch] = np.sin(angle) * (-1.0 if c % 2 == 0 else 1.0)
    headmask = (np.arange(P)[:, None] % 32 // HD == np.arange(HPR)[None]).astype(np.float32)
    e, j = np.meshgrid(np.arange(ROUTED), np.arange(ROUTED), indexing="ij")
    tiebreak = np.where(j < e, 0.0, MIN_NORMAL).astype(np.float32).reshape(-1)
    tiebreak = np.broadcast_to(np.tile(tiebreak, SUBS), (P, SUBS * ROUTED * ROUTED))
    const = np.concatenate([ident, cos, sin, headmask, tiebreak], axis=1)
    sel = np.zeros((CW_ROWS, ROUTED, P), np.float32)
    for part in range(3):
        for e in range(ROUTED):
            sel[part * ROUTED + e, e] = 1.0
    return np.ascontiguousarray(const), sel.reshape(CW_ROWS, ROUTED * P)


def windows(x):
    x = x.reshape(4, 2, 8, 2, 2, 8, 2, C)
    return x.transpose(0, 1, 4, 3, 6, 2, 5, 7).reshape(TOKENS, C)


def images(y):
    y = y.reshape(4, 2, 2, 2, 2, 8, 8, C)
    return y.transpose(0, 1, 5, 3, 2, 6, 4, 7).reshape(4, 32, 32, C)


def kernel(x, L0_conv_qkv_w, L0_conv_qkv_b, L0_conv_proj_w, L0_conv_proj_b, L0_ffn_gate_w, L0_ffn_gate_b,
           L0_ffn_sw1, L0_ffn_sb1, L0_ffn_sw2, L0_ffn_sb2, L0_ffn_rw1, L0_ffn_rb1, L0_ffn_rw2, L0_ffn_rb2):
    import concourse.bacc as _bacc
    from concourse.bass_utils import run_bass_kernel_spmd as _run

    A = np.asarray
    swap = np.arange(P).reshape(-1, 2)[:, ::-1].reshape(-1)
    qkv_w, qkv_b = A(L0_conv_qkv_w), A(L0_conv_qkv_b)
    q_w, k_w, v_w = qkv_w[0:P], qkv_w[P:2 * P], qkv_w[2 * P:]
    q_b, k_b, v_b = qkv_b[0:P], qkv_b[P:2 * P], qkv_b[2 * P:]
    const, sel = constants()
    w1 = np.concatenate([A(L0_ffn_sw1), A(L0_ffn_rw1)])
    w2 = np.concatenate([A(L0_ffn_sw2), A(L0_ffn_rw2)])
    b1 = np.concatenate([A(L0_ffn_sb1), A(L0_ffn_rb1)])
    up = w1.transpose(2, 0, 1).reshape(P, CHUNKS * P)
    down = w2.reshape(EXPERTS, C, FC, P).transpose(3, 0, 2, 1).reshape(P, CHUNKS * P)
    w12 = np.stack([up.reshape(P, EXPERTS, FC * P), down.reshape(P, EXPERTS, FC * P)], axis=2)
    w12 = w12.reshape(P, W_BLOCKS, W_BLOCK).transpose(1, 0, 2)
    b1 = b1.reshape(EXPERTS, FC, P).transpose(2, 0, 1).reshape(P, CHUNKS)
    arrays = {
        "x": windows(A(x)).reshape(TILES, SUBS, P, C).transpose(0, 2, 1, 3).reshape(TILES, P, TILE),
        "wqkv": np.concatenate([q_w.T, q_w[swap].T, k_w.T, k_w[swap].T, v_w.T, A(L0_conv_proj_w).T], axis=1),
        "bias": np.concatenate([q_b[:, None], q_b[swap][:, None], k_b[:, None], k_b[swap][:, None], v_b[:, None], b1],
                               axis=1),
        "const": const, "sel": sel,
        "proj_b": np.tile(A(L0_conv_proj_b), (P, 1)),
        "gate_w": A(L0_ffn_gate_w).T,
        "gate_b": np.tile(A(L0_ffn_gate_b), (P, SUBS)),
        "w12": w12,
        "b2": np.concatenate([np.tile(A(L0_ffn_rb2), (3, 1)), A(L0_ffn_sb2)]),
    }
    nc = _bacc.Bacc("TRN2", target_bir_lowering=False, num_devices=1)
    d, ins = {}, {}
    for name, a in arrays.items():
        ins[f"{name}_dram"] = a = np.ascontiguousarray(a)
        d[name] = nc.dram_tensor(f"{name}_dram", a.shape, mybir.dt.from_np(a.dtype), kind="ExternalInput").ap()
    d["yT"] = nc.dram_tensor("out_0_dram", (C, TOKENS), F32, kind="ExternalOutput").ap()
    build(nc, d)
    r = _run(nc, [ins], core_ids=[0])
    return images(r.results[0]["out_0_dram"].T)
```

```python
from contextlib import ExitStack

import numpy as np

import concourse.bass as bass
from concourse import mybir

F32 = mybir.dt.float32
F32R = mybir.dt.float32r
BF16 = mybir.dt.bfloat16
ALU = mybir.AluOpType
ACT = mybir.ActivationFunctionType
AX = mybir.AxisListType

P = 128
C = 128
TOKENS = 4096
TILE = 512
TILES = TOKENS // TILE
SUBS = TILE // P
WIN = 64
SEQS = TILE // WIN
HEADS, HD = 16, 8
SCALE = HD ** -0.5
HPR = 4
UNITS = 4
SHARED, ROUTED, TOPK = 2, 8, 2
EXPERTS = SHARED + ROUTED
FC = 4
CHUNKS = EXPERTS * FC
CW_ROWS = 3 * ROUTED + SHARED
SH = SHARED * FC
EPS_CONV, EPS_FFN = 1e-6, 1e-5
MIN_NORMAL = 1.1754944e-38
W_COLS = 2 * CHUNKS * P
W_BLOCK = TILE
W_BLOCKS = W_COLS // W_BLOCK

LAG = 6
STEPS = CHUNKS + LAG
CWT = 1
Q, QS, K, KS, V = 3, 3, 4, 5, (7, 8)
BEFORE_DOWN = ()
SCORES = (10, 14, 19, 22)
SHIFTS = (9, 14, 18, 22)
EXPS = (18, 18, 23, 23)
SUMS = (17, 20, 25, 27)
NORMS = (16, 18, 26, 26)
VALUES = (20, 23, 28, 30)
PROJ, X2T = 33, 38
STD2, NORM2, XN2T = 32, 37, 39
GATE, GATE_EXP, GATE_END = 41, 41, 42
X_LOW = 40
BIAS_X = 0
LN1, STD1, NORM1, XNT = 31, 36, 42, 45

FIRST_SCORES = (9, 11, 12, 13)
FIRST_SHIFTS = (9, 10, 12, 14)
FIRST_EXPS = (8, 11, 13, 17)
FIRST_SUMS = (10, 12, 14, 16)
FIRST_NORMS = (11, 12, 14, 16)
FIRST_VALUES = (12, 15, 18, 20)
W_STEPS = (1, 1, 5, 6, 10, 10, 13, 13, 16, 17, 19, 21, 24, 27, 31, 32, 32, 35, 39, 39)
WARM = {3: 4, 4: 4, 5: 4, 7: 4, 8: 4, 9: 4, 10: 4, 12: 4, 13: 4, 14: 4, 15: 4, 16: 4, 17: 4, 18: 4, 19: 4, 20:
        4, 21: 4, 22: 4, 23: 4, 33: 4, 38: 4, 39: 3, 41: 4}
WARM_SETUP = 4

QKV_BLOCKS = 6
CONST_COLS = {"ident": P, "cos": WIN, "sin": WIN, "headmask": HPR, "tiebreak": SUBS * ROUTED * ROUTED}
BIAS_COLS = {"q": 1, "qs": 1, "k": 1, "ks": 1, "v": 1, "b1": CHUNKS}


def offsets(cols):
    at, out = 0, {}
    for name, n in cols.items():
        out[name] = slice(at, at + n)
        at += n
    return out, at


CONST_AT, CONST_N = offsets(CONST_COLS)
BIAS_AT, BIAS_N = offsets(BIAS_COLS)


def at(tile, per_tile, k):
    return tile * per_tile + k


def wait(eng, sem, value):
    if isinstance(value, int) and value <= 0:
        return
    eng.wait_ge(sem, value)


def is_first(t):
    return isinstance(t, int) and t == 0


def tile_of(tensor, n):
    if isinstance(n, int):
        return tensor[n]
    return tensor[bass.ds(n, 1), :, :].rearrange("o p n -> p (o n)")


def build(nc, d):
    RING, M_RING, UP_BANKS = 8, 5, 3
    DVE_SHARE = (1, 3)
    DVE_LOWS = EXPERTS * len(DVE_SHARE)
    POOL_LOWS = CHUNKS - DVE_LOWS
    BANK = 12
    (B_CWT, B_V0, B_V1, B_PV0, B_PV1, B_PV2, B_PV3, B_PROJ, B_X2T, B_XN2T, B_GATE,
     B_XNT) = range(BANK)
    STAGES = 4
    GROUPS = 1 + ROUTED
    GATE_STEPS, LSHIFT, CW_FIRST = 10, 3, 10
    SETUP_DMAS, POOL_FILLS, DVE_CASTS = 8, 6, 6

    with ExitStack() as ctx:
        def sb(name, shape, dt=F32):
            return ctx.enter_context(nc.sbuf_tensor(name, shape, dt))

        def psum(name, shape):
            return ctx.enter_context(nc.psum_tensor(name, shape, F32))

        def sem(name):
            return ctx.enter_context(nc.semaphore(name))

        scores_ps = psum("scores_ps", [P, 1024])
        spread_ps = psum("spread_ps", [P, TILE])
        shared_ps = psum("shared_ps", [P, TILE])
        up_ps = [psum(f"up_ps{i}", [P, TILE]) for i in range(UP_BANKS)]
        z_ps = psum("z_ps", [P, TILE])

        const, biases = sb("const", [P, CONST_N]), sb("biases", [P, BIAS_N])
        b2, b2_parts = sb("b2", [CW_ROWS, P]), sb("b2_parts", [CW_ROWS, 3, P], BF16)
        sel = sb("sel", [CW_ROWS, ROUTED, P], BF16)
        w_hi, w_lo = sb("w_hi", [P, W_COLS], F32R), sb("w_lo", [P, W_COLS], F32R)
        wqkv = sb("wqkv", [P, QKV_BLOCKS * P])
        gate_w = sb("gate_w", [P, ROUTED])
        gate_b = sb("gate_b", [P, SUBS * ROUTED])
        proj_b = sb("proj_b", [P, C])
        half_neg = sb("half_neg", [P, SUBS])
        eps_conv, eps_ffn = sb("eps_conv", [P, SUBS]), sb("eps_ffn", [P, SUBS])
        ident_bf = sb("ident_bf", [P, P], BF16)
        x_in, x_res = sb("x_in", [P, TILE]), sb("x_res", [P, TILE])
        stats, stats2 = sb("stats", [P, SUBS, 6]), sb("stats2", [P, SUBS, 6])
        stats_seen, table_seen = sb("stats_seen", [P, 1]), sb("table_seen", [P, 2])
        mv1, mv2 = sb("mv1", [P, SUBS, 2]), sb("mv2", [P, SUBS, 2])
        ve1, ve2 = sb("ve1", [P, SUBS]), sb("ve2", [P, SUBS])
        rstd1, rstd2 = sb("rstd1", [P, SUBS]), sb("rstd2", [P, SUBS])
        xn, xnT = sb("xn", [P, TILE]), sb("xnT", [P, TILE])
        q_rot, k_rot, sines = sb("q_rot", [P, TILE]), sb("k_rot", [P, TILE]), sb("sines", [P, TILE])
        k_masked = sb("k_masked", [P, SEQS, HPR, WIN])
        v_spread = sb("v_spread", [P, SEQS * (HEADS // 2) * 32 + 32])
        smax, psums, rinv = (sb(n, [P, UNITS, 16]) for n in ("smax", "psums", "rinv"))
        probs = [sb(f"probs{i}", [P, 1024]) for i in range(UNITS)]
        probsT = [sb(f"probsT{i}", [P, 4, P]) for i in range(2)]
        attnT = sb("attnT", [P, TILE])
        x2 = sb("x2", [P, TILE])
        x2T = sb("x2T", [P, 2 * TILE])
        G = [P, SUBS, ROUTED]
        logits, lshift, lexp = sb("logits", G), sb("lshift", G), sb("lexp", G)
        lmax, lsum, linv = (sb(n, [P, SUBS]) for n in ("lmax", "lsum", "linv"))
        pairdiff = sb("pairdiff", [P, SUBS, ROUTED, ROUTED])
        beats = sb("beats", [P, SUBS, ROUTED, ROUTED])
        rank, chosen, cw, cw_rest = sb("rank", G), sb("chosen", G), sb("cw", G), sb("cw_rest", G)
        zeros = sb("zeros", G)
        cw_parts = sb("cw_parts", [P, SUBS, CW_ROWS], BF16)
        cwT = sb("cwT", [CW_ROWS, TILE], BF16)
        x_hi, x_lo = sb("x_hi", [P, TILE], F32R), sb("x_lo", [P, TILE], F32R)
        m = [sb(f"m{i}", [P, TILE]) for i in range(M_RING)]
        m_hi = [sb(f"m_hi{i}", [P, TILE], F32R) for i in range(RING)]
        m_lo = [sb(f"m_lo{i}", [P, TILE], F32R) for i in range(RING)]
        weighted = [sb(f"weighted{i}", [P, TILE]) for i in range(2)]
        y_sum = sb("y_sum", [P, TILE])
        cw_wide = sb("cw_wide", [P, TILE])

        constants_in, pool_fills, dve_casts = sem("constants_in"), sem("pool_fills"), sem("dve_casts")
        w_loaded = [sem(f"w_loaded{j}") for j in range(STAGES)]
        w_hi_ready, w_lo_ready = sem("w_hi_ready"), sem("w_lo_ready")
        x_loaded, xres_loaded = sem("x_loaded"), sem("xres_loaded")
        stats1_done, stats2_done = sem("stats1_done"), sem("stats2_done")
        ln1_done, rstd1_step, xn_ready = sem("ln1_done"), sem("rstd1_step"), sem("xn_ready")
        ln2_done, rstd2_step, xn2_ready = sem("ln2_done"), sem("rstd2_step"), sem("xn2_ready")
        bank_written, bank_read = sem("bank_written"), sem("bank_read")
        projected, rotated = sem("projected"), sem("rotated")
        q_ready, k_ready, k_masked_ready = sem("q_ready"), sem("k_ready"), sem("k_masked_ready")
        scores_done, max_done, shifted_ready = sem("scores_done"), sem("max_done"), sem("shifted_ready")
        probs_ready, sum_done, rinv_ready = sem("probs_ready"), sem("sum_done"), sem("rinv_ready")
        normed, transposed, probsT_ready = sem("normed"), sem("transposed"), sem("probsT_ready")
        scores_half = sem("scores_half")
        xres_biased, x2_ready = sem("xres_biased"), sem("x2_ready")
        gate_step, lexp_ready, cw_ready = sem("gate_step"), sem("lexp_ready"), sem("cw_ready")
        parts_step = sem("parts_step")
        x_hi_ready, x_lo_ready = sem("x_hi_ready"), sem("x_lo_ready")
        up_done, cw_spread, down_done = sem("up_done"), sem("cw_spread"), sem("down_done")
        cw_copied = sem("cw_copied")
        gelu_done, z_used, y_added = sem("gelu_done"), sem("z_used"), sem("y_added")
        hi_ready = sem("hi_ready")
        lo_by_dve, lo_by_pool = sem("lo_by_dve"), sem("lo_by_pool")
        y_stored = sem("y_stored")

        ident = const[:, CONST_AT["ident"]]
        cos, sin = const[:, CONST_AT["cos"]], const[:, CONST_AT["sin"]]
        headmask, tiebreak = const[:, CONST_AT["headmask"]], const[:, CONST_AT["tiebreak"]]

        def bias(name):
            return biases[:, BIAS_AT[name]]

        def up_weights(part, n):
            e, c = divmod(n, FC)
            return part[:, (2 * e * FC + c) * P:(2 * e * FC + c + 1) * P]

        def down_weights(part, n):
            e, c = divmod(n, FC)
            return part[:, ((2 * e + 1) * FC + c) * P:((2 * e + 1) * FC + c + 1) * P]

        def x2T_of(t):
            half = (t % 2) * TILE
            return x2T[:, half:half + TILE] if isinstance(t, int) else x2T[:, bass.ds(half, TILE)]

        def group(n):
            return 0 if n < SH else n // FC - SHARED + 1

        def wait_low_part(eng, t, n):
            tile, n = (t, n) if n >= 0 else (t - 1, n + CHUNKS)
            by_dve = sum(1 for i in range(n + 1) if i % FC in DVE_SHARE)
            if n % FC in DVE_SHARE:
                eng.wait_ge(lo_by_dve, at(tile, DVE_LOWS, by_dve))
            else:
                eng.wait_ge(lo_by_pool, at(tile, POOL_LOWS, n + 1 - by_dve))

        def run_iterations(eng, body):
            body(0, False, True)
            with eng.Fori(1, TILES) as t:
                body(t, True, True)
            body(TILES, True, False)

        block = ctx.enter_context(nc.Block())

        @block.sync
        def _(sp):
            sp.dma_start(x_in[:], d["x"][0]).then_inc(x_loaded, 16)
            sp.dma_start(const[:], d["const"]).then_inc(constants_in, 16)
            sp.dma_start(wqkv[:], d["wqkv"]).then_inc(constants_in, 16)
            sp.dma_start(biases[:], d["bias"]).then_inc(constants_in, 16)
            sp.dma_start(gate_w[:], d["gate_w"]).then_inc(constants_in, 16)
            sp.dma_start(gate_b[:], d["gate_b"]).then_inc(constants_in, 16)
            sp.dma_start(proj_b[:], d["proj_b"]).then_inc(constants_in, 16)
            sp.dma_start(b2[:], d["b2"]).then_inc(constants_in, 16)
            sp.dma_start(probs[3][0:CW_ROWS, :], d["sel"]).then_inc(constants_in, 16)
            sp.dma_start(x_res[:], d["x"][0]).then_inc(xres_loaded, 16)

            def load_x(t):
                sp.wait_ge(xn_ready, at(t - 1, 1, 1))
                sp.dma_start(x_in[:], tile_of(d["x"], t % TILES)).then_inc(x_loaded, 16)

            load_x(1)
            for n in range(W_BLOCKS):
                wait(sp, w_lo_ready, n - STAGES + 1)
                sp.dma_start(m[n % STAGES][:], d["w12"][n]).then_inc(w_loaded[n % STAGES], 16)
            sp.sem_inc(y_stored, 16)

            def body(t, experts, attend):
                if attend:
                    wait(sp, x2_ready, at(t, 1, 1))
                    sp.dma_start(x_res[:], tile_of(d["x"], (t + 1) % TILES)).then_inc(xres_loaded, 16)
                if experts:
                    sp.wait_ge(y_added, at(t, ROUTED, ROUTED))
                    cols = slice((t - 1) * TILE, t * TILE) if isinstance(t, int) else bass.ds((t - 1) * TILE, TILE)
                    sp.dma_start(d["yT"][:, cols], y_sum[:]).then_inc(y_stored, 16)
                if attend:
                    load_x(t + 2)

            run_iterations(sp, body)
            sp.wait_ge(y_stored, 16 * (TILES + 1))

        @block.tensor
        def _(pe):
            def use_bank(t, use):
                wait(pe, bank_read, at(t, BANK, use))

            def transposes(t, use, src):
                use_bank(t, use)
                for s in range(SUBS):
                    mm = nc.tensor.transpose(shared_ps[:, s * P:(s + 1) * P], src[:, s * P:(s + 1) * P], ident)
                mm.then_inc(bank_written, 1)

            def project(t, b):
                if b < 2:
                    wait(pe, shifted_ready, at(t, UNITS, 0))
                else:
                    wait(pe, rotated, at(t, 4, b - 1))
                if b == 0:
                    pe.wait_ge(bank_read, at(t, BANK, 1))
                nc.tensor.matmul(scores_ps[:, b % 2 * TILE:(b % 2 + 1) * TILE], wqkv[:, b * P:(b + 1) * P], xnT[:],
                                 start=True, stop=True).then_inc(projected, 1)

            def project_v(t, quad):
                use_bank(t, B_V0 + quad)
                for s in range(4):
                    seq = quad * 4 + s
                    for h2 in range(2):
                        mm = nc.tensor.matmul(shared_ps[64 * h2:64 * h2 + 64, s * P:(s + 1) * P],
                                              xnT[:, seq * WIN:(seq + 1) * WIN],
                                              wqkv[:, 4 * P:5 * P], start=True, stop=True)
                mm.then_inc(bank_written, 1)

            def scores(t, u, half):
                if u == 0 and half == 0:
                    wait(pe, q_ready, at(t, 1, 1))
                    wait(pe, k_masked_ready, at(t, 1, 1))
                if half == 0:
                    wait(pe, shifted_ready, at(t, UNITS, u))
                else:
                    pe.wait_ge(scores_half, at(t, UNITS, u + 1))
                for i, s in ((0, 0), (1, 1), (0, 1), (1, 0)):
                    seq, rg = 2 * u + s, 2 * half + i
                    rows = slice(32 * rg, 32 * rg + 32)
                    c0 = i * 512 + half * 256
                    mm = nc.tensor.matmul(
                        scores_ps[64 * s:64 * s + 64, c0:c0 + 256], q_rot[rows, seq * WIN:(seq + 1) * WIN],
                        k_masked[rows, seq, :, :].rearrange("p h m -> p (h m)"), start=True, stop=True)
                mm.then_inc(scores_half if half == 0 else scores_done, 1)

            def probs_transposes(t, u, pair):
                wait(pe, normed, at(t, UNITS, u + 1))
                spreads = sum(1 for e in range(SHARED, EXPERTS) if e * FC + LAG < VALUES[u] + pair)
                wait(pe, cw_copied, at(t, ROUTED, spreads))
                wait(pe, probsT_ready, at(t, 2 * UNITS, 2 * u + pair))
                for b in range(4):
                    c0 = pair * 512 + b * P
                    mm = nc.tensor.transpose(spread_ps[:, b * P:(b + 1) * P], probs[u][:, c0:c0 + P], ident)
                mm.then_inc(transposed, 1)

            def values(t, u):
                use_bank(t, B_PV0 + u)
                wait(pe, probsT_ready, at(t, 2 * UNITS, 2 * u + 2))
                for s in range(2):
                    for h2 in range(2):
                        for rg in range(HEADS // HPR):
                            c0 = 16 + ((2 * u + s) * (HEADS // 2) + 2 * rg + h2) * 32 - 16 * h2
                            mm = nc.tensor.matmul(shared_ps[32 * rg:32 * rg + 32, s * WIN:(s + 1) * WIN],
                                                  v_spread[:, c0:c0 + 32],
                                                  probsT[rg % 2][:, 2 * (rg // 2) + h2, s * WIN:(s + 1) * WIN],
                                                  start=(h2 == 0), stop=(h2 == 1), skip_group_check=True)
                mm.then_inc(bank_written, 1)

            def out_projection(t):
                use_bank(t, B_PROJ)
                for s in range(SUBS):
                    mm = nc.tensor.matmul(shared_ps[:, s * P:(s + 1) * P], attnT[:, s * P:(s + 1) * P],
                                          wqkv[:, 5 * P:6 * P], start=True, stop=True)
                mm.then_inc(bank_written, 1)

            def gate(t):
                use_bank(t, B_GATE)
                for s in range(SUBS):
                    mm = nc.tensor.matmul(shared_ps[:, s * ROUTED:(s + 1) * ROUTED], xnT[:, s * P:(s + 1) * P],
                                          gate_w[:], start=True, stop=True)
                mm.then_inc(bank_written, 1)

            def combine_weights(t):
                wait(pe, cw_ready, at(t, 1, 1))
                use_bank(t + 1, B_CWT)
                for s in range(SUBS):
                    mm = nc.tensor.transpose(shared_ps[:].bitcast(BF16)[0:CW_ROWS, s * P:(s + 1) * P],
                                             cw_parts[:, s, :], ident_bf[:])
                mm.then_inc(bank_written, 1)

            def attention(t, n):
                if n == XNT:
                    wait(pe, xn_ready, at(t + 1, 1, 1))
                    transposes(t, B_XNT, xn)
                for b, step in enumerate((Q, QS, K, KS)):
                    if n == step:
                        project(t, b)
                for quad in range(2):
                    if n == V[quad]:
                        project_v(t, quad)
                values_at = FIRST_VALUES if is_first(t) else VALUES
                for u in range(UNITS):
                    if n == values_at[u] + 2:
                        values(t, u)
                    for pair in range(2):
                        if n == values_at[u] + pair:
                            probs_transposes(t, u, pair)
                if n == PROJ:
                    out_projection(t)
                if n == X2T:
                    wait(pe, x2_ready, at(t, 1, 1))
                    transposes(t, B_X2T, x2)
                if n == XN2T:
                    wait(pe, xn2_ready, at(t, 1, 1))
                    transposes(t, B_XN2T, xn)
                if n == GATE:
                    gate(t)

            def three_passes(out, weights, n, hi, lo, start, stop):
                nc.tensor.matmul(out, weights(w_hi, n), hi, start=start, stop=False, skip_group_check=True)
                nc.tensor.matmul(out, weights(w_hi, n), lo, start=False, stop=False, skip_group_check=True)
                return nc.tensor.matmul(out, weights(w_lo, n), hi, start=False, stop=stop, skip_group_check=True)

            def up(t, n):
                last = n - UP_BANKS if n >= UP_BANKS else max(i for i in range(CHUNKS) if i % UP_BANKS == n) - CHUNKS
                pe.wait_ge(gelu_done, at(t, CHUNKS, last + 1))
                three_passes(up_ps[n % UP_BANKS][:], up_weights, n, x_hi[:], x_lo[:], True, True).then_inc(up_done, 1)

            def spread_cw(t, e, attend):
                pe.wait_ge(cw_copied, at(t, ROUTED, e - SHARED))
                copied = sum(1 for v in VALUES for pair in range(2) if v + pair <= e * FC + LAG)
                if attend and copied > 0:
                    pe.wait_ge(probsT_ready, at(t, 2 * UNITS, copied))
                nc.tensor.matmul(spread_ps[:], sel[:, e - SHARED, :], cwT[:],
                                 start=True, stop=True).then_inc(cw_spread, 1)

            def out_biases(t):
                pe.wait_ge(z_used, at(t, GROUPS, 0))
                for part in range(3):
                    nc.tensor.matmul(z_ps[:], b2_parts[:, part, :], cwT[:],
                                     start=(part == 0), stop=False, skip_group_check=True)

            def down(t, n, attend):
                first = n >= SH and n % FC == 0
                if first:
                    pe.wait_ge(z_used, at(t, GROUPS, group(n)))
                wait_low_part(pe, t, n)
                three_passes(z_ps[:], down_weights, n, m_hi[n % RING][:], m_lo[n % RING][:], first,
                             n >= SH - 1 and n % FC == FC - 1).then_inc(down_done, 1)
                if first:
                    spread_cw(t, n // FC, attend)

            def keep_warm(times):
                for _ in range(times):
                    nc.tensor.matmul(up_ps[0][:, 0:P], ident, ident, start=True, stop=True)

            def body(t, experts, attend):
                if experts:
                    pe.wait_ge(x_lo_ready, at(t, 1, 0))
                for n in range(STEPS):
                    if experts:
                        if n < CHUNKS:
                            up(t, n)
                        if n == CWT:
                            combine_weights(t - 1)
                        if n == LAG:
                            pe.wait_ge(bank_read, at(t, BANK, B_CWT + 1))
                            out_biases(t)
                    new_group = n - LAG >= SH and (n - LAG) % FC == 0
                    scores_at = FIRST_SCORES if is_first(t) else SCORES
                    if attend and n in scores_at:
                        scores(t, scores_at.index(n), 0)
                    before = new_group or n in BEFORE_DOWN
                    if attend and before:
                        attention(t, n)
                    if experts and n >= LAG:
                        down(t, n - LAG, attend)
                    if attend and n in scores_at:
                        scores(t, scores_at.index(n), 1)
                    if attend and not before:
                        attention(t, n)
                    if not experts:
                        keep_warm(WARM.get(n, 0))

            pe.sem_inc(up_done, CHUNKS)
            pe.sem_inc(cw_spread, ROUTED)
            pe.sem_inc(down_done, CHUNKS)
            pe.wait_ge(constants_in, 16 * SETUP_DMAS)
            keep_warm(WARM_SETUP)
            pe.wait_ge(xn_ready, 1)
            transposes(0, B_CWT, xn)
            pe.wait_ge(pool_fills, POOL_FILLS)
            pe.wait_ge(dve_casts, DVE_CASTS)
            body(0, False, True)
            pe.wait_ge(w_lo_ready, W_BLOCKS)
            with pe.Fori(1, TILES) as t:
                body(t, True, True)
            body(TILES, True, False)

        @block.scalar
        def _(act):
            def from_bank(t, use, out, inp):
                wait(act, bank_written, at(t, BANK, use + 1))
                nc.scalar.copy(out, inp).then_inc(bank_read, 1)

            def load_table(function, column):
                nc.scalar.activation(table_seen[:, column:column + 1], half_neg[:, 0:1], function)

            def exp(t, u):
                wait(act, shifted_ready, at(t, UNITS, u + 1))
                nc.scalar.activation(probs[u][:], probs[u][:], ACT.Exp, scale=SCALE).then_inc(probs_ready, 1)

            def copy_probsT(t, u, pair):
                wait(act, transposed, at(t, 2 * UNITS, 2 * u + pair + 1))
                if u > 0:
                    wait(act, bank_written, at(t, BANK, B_PV0 + u))
                nc.scalar.copy(probsT[pair][:].rearrange("p b n -> p (b n)"), spread_ps[:]).then_inc(probsT_ready, 1)

            def copy_attn(t, u):
                wait(act, bank_written, at(t, BANK, B_PV0 + u + 1))
                nc.scalar.activation(attnT[:, u * P:(u + 1) * P], shared_ps[:, 0:P], ACT.Identity,
                                     bias=bias("v")).then_inc(bank_read, 1)

            def mask_k(t, h):
                if h == 0:
                    wait(act, k_ready, at(t, 1, 1))
                    wait(act, scores_done, at(t, UNITS, 0))
                op = nc.scalar.mul(k_masked[:, :, h, :], k_rot[:].rearrange("p (s m) -> p s m", s=SEQS),
                                   headmask[:, h:h + 1])
                if h == HPR - 1:
                    op.then_inc(k_masked_ready, 1)

            def spread_v(t, quad):
                wait(act, bank_written, at(t, BANK, B_V0 + quad + 1))
                for h2 in range(2):
                    rows = slice(64 * h2, 64 * h2 + 64)
                    groups = 4 * HEADS // 2
                    dst = v_spread[rows, 16 + quad * groups * 32:16 + (quad + 1) * groups * 32].rearrange(
                        "p (g w) -> p g w", w=32)[:, :, h2 * HD:(h2 + 1) * HD]
                    src = shared_ps[rows, :].rearrange("p (g w) -> p g w", w=16)[:, :, h2 * HD:(h2 + 1) * HD]
                    op = nc.scalar.copy(dst, src)
                op.then_inc(bank_read, 1)

            def attention(t, n):
                if n == XNT:
                    act.wait_ge(x_lo_ready, at(t, 1, 1))
                    from_bank(t, B_XNT, xnT[:], shared_ps[:])
                for quad in range(2):
                    if n == V[quad]:
                        spread_v(t, quad)
                        mask_k(t, 2 * quad)
                        mask_k(t, 2 * quad + 1)
                exps_at, values_at = (FIRST_EXPS, FIRST_VALUES) if is_first(t) else (EXPS, VALUES)
                for u in range(UNITS):
                    if n == exps_at[u]:
                        exp(t, u)
                for u in range(UNITS):
                    if n == values_at[u] + 2:
                        copy_attn(t, u)
                    for pair in range(2):
                        if n == values_at[u] + pair:
                            copy_probsT(t, u, pair)
                if n == X2T:
                    from_bank(t, B_X2T, x2T_of(t), shared_ps[:])
                if n == XN2T:
                    from_bank(t, B_XN2T, xnT[:], shared_ps[:])
                if n == GATE_EXP:
                    load_table(ACT.Exp, 0)
                    wait(act, gate_step, at(t, GATE_STEPS, LSHIFT))
                    nc.scalar.activation(lexp[:], lshift[:], ACT.Exp).then_inc(lexp_ready, 1)
                    load_table(ACT.Gelu, 1)

            def gelu(t, n):
                act.wait_ge(up_done, at(t, CHUNKS, n + 1))
                wait_low_part(act, t, n - M_RING)
                nc.scalar.activation(m[n % M_RING][:], up_ps[n % UP_BANKS][:], ACT.Gelu,
                                     bias=bias("b1")[:, n:n + 1]).then_inc(gelu_done, 1)

            def copy_cw(t, e):
                act.wait_ge(cw_spread, at(t, ROUTED, e - SHARED + 1))
                nc.scalar.copy(cw_wide[:], spread_ps[:]).then_inc(cw_copied, 1)

            def weights_high(n):
                act.wait_ge(w_loaded[n % STAGES], 16 * (n // STAGES + 1))
                nc.scalar.copy(w_hi[:, n * W_BLOCK:(n + 1) * W_BLOCK], m[n % STAGES][:]).then_inc(w_hi_ready, 1)

            def body(t, experts, attend):
                for n in range(STEPS):
                    if experts:
                        if n < CHUNKS:
                            gelu(t, n)
                        if n == CWT:
                            wait(act, bank_written, at(t, BANK, B_CWT + 1))
                            act.wait_ge(cw_spread, at(t, ROUTED, 0))
                            nc.scalar.copy(cwT[:], shared_ps[:].bitcast(BF16)[0:CW_ROWS, 0:TILE])\
                                .then_inc(bank_read, 1)
                    if attend:
                        attention(t, n)
                    if experts and n - LAG >= SH and (n - LAG) % FC == 0:
                        copy_cw(t, (n - LAG) // FC)
                    if attend and n == CHUNKS:
                        if experts:
                            act.wait_ge(up_done, at(t, CHUNKS, CHUNKS))
                        act.wait_ge(bank_read, at(t, BANK, B_XN2T + 1))
                        nc.scalar.copy(x_hi[:], xnT[:]).then_inc(x_hi_ready, 1)
                    for block_n in range(W_BLOCKS):
                        if not experts and n == W_STEPS[block_n]:
                            weights_high(block_n)

            act.sem_inc(gelu_done, CHUNKS)
            act.sem_inc(cw_copied, ROUTED)
            act.wait_ge(constants_in, 16 * SETUP_DMAS)
            act.wait_ge(pool_fills, POOL_FILLS)
            from_bank(0, B_CWT, xnT[:], shared_ps[:])
            body(0, False, True)
            with act.Fori(1, TILES) as t:
                body(t, True, True)
            body(TILES, True, False)

        @block.vector
        def _(dve):
            def row_stats(src, raw, done, begun=None):
                for s in range(SUBS):
                    op = nc.vector.bn_stats(raw[:, s, :], src[:, s * P:(s + 1) * P])
                    if s == 0 and begun is not None:
                        op.then_inc(begun, 1)
                op.then_inc(done, 1)

            def merge_stats(t, stats_done, raw, mv, done):
                wait(dve, stats_done, at(t, 1, 1))
                nc.vector.tensor_copy(stats_seen[:], raw[:, 0, 0:1])
                for s in range(SUBS):
                    op = nc.vector.bn_aggr(mv[:, s, :], raw[:, s, :])
                op.then_inc(done, 1)

            def normalise_rows(t, src, mv, rstd, out, step, ready):
                wait(dve, step, at(t, 2, 2))
                for s in range(SUBS):
                    op = nc.vector.tensor_scalar(out[:, s * P:(s + 1) * P], src[:, s * P:(s + 1) * P], mv[:, s, 0:1],
                                                 rstd[:, s:s + 1], ALU.subtract, ALU.mult)
                op.then_inc(ready, 1)

            def rotate(t, which, out, b, table):
                wait(dve, projected, at(t, 4, which + 1))
                nc.vector.scalar_tensor_tensor(
                    out=out[:].rearrange("p (s m) -> p s m", m=WIN),
                    in0=scores_ps[:, which % 2 * TILE:(which % 2 + 1) * TILE].rearrange("p (s m) -> p s m", m=WIN),
                    scalar=bias(b), in1=table.unsqueeze(1).broadcast_to([P, SEQS, WIN]),
                    op0=ALU.add, op1=ALU.mult).then_inc(rotated, 1)

            def shift(t, u):
                grid = scores_ps[:].rearrange("p (g m) -> p g m", m=WIN)
                wait(dve, scores_done, at(t, UNITS, u + 1))
                nc.vector.tensor_reduce(smax[:, u, :], grid, AX.X, ALU.max).then_inc(max_done, 1)
                wait(dve, max_done, at(t, UNITS, u + 1))
                wait(dve, transposed, at(t - 1, 2 * UNITS, 2 * u + 2))
                nc.vector.tensor_tensor(probs[u][:].rearrange("p (g m) -> p g m", m=WIN), grid,
                                        smax[:, u, :].unsqueeze(2).broadcast_to([P, 16, WIN]),
                                        ALU.subtract).then_inc(shifted_ready, 1)

            def sums(t, u):
                wait(dve, probs_ready, at(t, UNITS, u + 1))
                nc.vector.tensor_reduce(psums[:, u, :], probs[u][:].rearrange("p (g m) -> p g m", m=WIN),
                                        AX.X, ALU.add).then_inc(sum_done, 1)
                wait(dve, sum_done, at(t, UNITS, u + 1))
                nc.vector.reciprocal(rinv[:, u, :], psums[:, u, :]).then_inc(rinv_ready, 1)

            def residual(t):
                wait(dve, bank_written, at(t, BANK, B_PROJ + 1))
                wait(dve, xres_biased, at(t, 1, 1))
                nc.vector.tensor_tensor(x2[:], shared_ps[:], x_res[:], ALU.add).then_inc(bank_read, 1)
                wait(dve, bank_read, at(t, BANK, B_PROJ + 1))
                row_stats(x2, stats2, stats2_done, begun=x2_ready)

            def gate_first(t):
                wait(dve, bank_written, at(t, BANK, B_GATE + 1))
                nc.vector.tensor_tensor(logits[:].rearrange("p s e -> p (s e)"), shared_ps[:, 0:SUBS * ROUTED],
                                        gate_b[:], ALU.add).then_inc(bank_read, 1)
                wait(dve, bank_read, at(t, BANK, B_GATE + 1))
                nc.vector.tensor_reduce(lmax[:], logits[:], AX.X, ALU.max).then_inc(gate_step, 1)
                e_of_j = logits[:].unsqueeze(2).broadcast_to([P, SUBS, ROUTED, ROUTED])
                e_own = logits[:].unsqueeze(3).broadcast_to([P, SUBS, ROUTED, ROUTED])
                nc.vector.tensor_tensor(pairdiff[:], e_of_j, e_own, ALU.subtract).then_inc(gate_step, 1)
                wait(dve, gate_step, at(t, GATE_STEPS, 2))
                nc.vector.tensor_tensor(lshift[:], logits[:], lmax[:].unsqueeze(2).broadcast_to(G),
                                        ALU.subtract).then_inc(gate_step, 1)
                nc.vector.tensor_tensor(beats[:].rearrange("p s e j -> p (s e j)"),
                                        pairdiff[:].rearrange("p s e j -> p (s e j)"), tiebreak,
                                        ALU.is_ge).then_inc(gate_step, 1)
                wait(dve, gate_step, at(t, GATE_STEPS, 4))
                nc.vector.tensor_reduce(rank[:], beats[:], AX.X, ALU.add).then_inc(gate_step, 1)

            def gate_second(t):
                wait(dve, lexp_ready, at(t, 1, 1))
                nc.vector.tensor_reduce(lsum[:], lexp[:], AX.X, ALU.add).then_inc(gate_step, 1)
                wait(dve, gate_step, at(t, GATE_STEPS, 6))
                nc.vector.reciprocal(linv[:], lsum[:]).then_inc(gate_step, 1)
                nc.vector.scalar_tensor_tensor(out=chosen[:], in0=rank[:], scalar=TOPK - 0.5, in1=lexp[:],
                                               op0=ALU.is_lt, op1=ALU.mult).then_inc(gate_step, 1)
                wait(dve, gate_step, at(t, GATE_STEPS, 8))
                nc.vector.tensor_tensor(cw[:], chosen[:], linv[:].unsqueeze(2).broadcast_to(G),
                                        ALU.mult).then_inc(gate_step, 1)
                wait(dve, gate_step, at(t, GATE_STEPS, 9))
                nc.vector.tensor_copy(cw_parts[:, :, 0:ROUTED], cw[:]).then_inc(gate_step, 1)

            def first_stats(t):
                wait(dve, x_loaded, at(t, 16, 16))
                row_stats(x_in, stats, stats1_done)
                merge_stats(t, stats1_done, stats, mv1, ln1_done)

            def attention(t, n):
                if n == LN1:
                    first_stats(t + 1)
                if n == NORM1:
                    normalise_rows(t + 1, x_in, mv1, rstd1, xn, rstd1_step, xn_ready)
                for which, (step, out, b, table) in enumerate(((Q, q_rot, "q", cos), (QS, sines, "qs", sin),
                                                               (K, k_rot, "k", cos), (KS, sines, "ks", sin))):
                    if n == step:
                        if step == KS:
                            wait(dve, q_ready, at(t, 1, 1))
                        rotate(t, which, out, b, table)
                for u in range(UNITS):
                    if n == (FIRST_SHIFTS if is_first(t) else SHIFTS)[u]:
                        shift(t, u)
                for u in range(UNITS):
                    if n == (FIRST_SUMS if is_first(t) else SUMS)[u]:
                        sums(t, u)
                if n == PROJ:
                    residual(t)
                    merge_stats(t, stats2_done, stats2, mv2, ln2_done)
                if n == NORM2:
                    normalise_rows(t, x2, mv2, rstd2, xn, rstd2_step, xn2_ready)
                if n == GATE:
                    gate_first(t)
                if n == GATE_END:
                    gate_second(t)

            def weigh(t, g):
                last = SH if g == 0 else SH + g * FC
                dve.wait_ge(down_done, at(t, CHUNKS, last))
                if g == 0:
                    dve.wait_ge(y_stored, at(t, 16, 0))
                    nc.vector.tensor_tensor(y_sum[:], z_ps[:], x2T_of(t - 1), ALU.add).then_inc(z_used, 1)
                else:
                    dve.wait_ge(cw_copied, at(t, ROUTED, g))
                    dve.wait_ge(y_added, at(t, ROUTED, g - 2))
                    nc.vector.tensor_tensor(weighted[g % 2][:], z_ps[:], cw_wide[:], ALU.mult).then_inc(z_used, 1)

            def high_part(t, n):
                dve.wait_ge(gelu_done, at(t, CHUNKS, n + 1))
                dve.wait_ge(down_done, at(t, CHUNKS, n - RING + 1))
                nc.vector.tensor_copy(m_hi[n % RING][:], m[n % M_RING][:]).then_inc(hi_ready, 1)

            def low_part(t, n):
                dve.wait_ge(hi_ready, at(t, CHUNKS, n + 1))
                nc.vector.tensor_tensor(m_lo[n % RING][:], m[n % M_RING][:], m_hi[n % RING][:].bitcast(F32),
                                        ALU.subtract).then_inc(lo_by_dve, 1)

            def body(t, experts, attend):
                for n in range(STEPS):
                    if experts:
                        ended = n - LAG
                        if ended >= SH - 1 and ended % FC == FC - 1:
                            weigh(t, group(ended))
                        if n < CHUNKS:
                            high_part(t, n)
                        if 0 <= n - 1 < CHUNKS and (n - 1) % FC in DVE_SHARE:
                            low_part(t, n - 1)
                    if attend:
                        attention(t, n)

            dve.sem_inc(hi_ready, CHUNKS)
            dve.sem_inc(lo_by_dve, DVE_LOWS)
            dve.sem_inc(z_used, GROUPS)
            first_stats(0)
            normalise_rows(0, x_in, mv1, rstd1, xn, rstd1_step, xn_ready)
            dve.wait_ge(constants_in, 16 * SETUP_DMAS)
            nc.vector.tensor_copy(ident_bf[:], ident).then_inc(dve_casts, 1)
            nc.vector.tensor_copy(sel[:].rearrange("p e n -> p (e n)"), probs[3][0:CW_ROWS, :]).then_inc(dve_casts, 1)
            nc.vector.tensor_copy(b2_parts[:, 0, :], b2[:]).then_inc(dve_casts, 1)
            dve.wait_ge(dve_casts, 3)
            nc.vector.tensor_tensor(b2[:], b2[:], b2_parts[:, 0, :], ALU.subtract).then_inc(dve_casts, 1)
            dve.wait_ge(dve_casts, 4)
            nc.vector.tensor_copy(b2_parts[:, 1, :], b2[:]).then_inc(dve_casts, 1)
            dve.wait_ge(dve_casts, 5)
            nc.vector.tensor_tensor(b2_parts[:, 2, :], b2[:], b2_parts[:, 1, :], ALU.subtract).then_inc(dve_casts, 1)
            run_iterations(dve, body)

        @block.gpsimd
        def _(pool):
            def inverse_std(t, mv, ve, rstd, eps, done, step):
                wait(pool, done, at(t, 1, 1))
                nc.gpsimd.tensor_tensor(ve[:], mv[:, :, 1], eps[:], ALU.add).then_inc(step, 1)
                wait(pool, step, at(t, 2, 1))
                nc.gpsimd.tensor_tensor(rstd[:], ve[:], half_neg[:], ALU.pow).then_inc(step, 1)

            def normalise(t, u):
                wait(pool, rinv_ready, at(t, UNITS, u + 1))
                grid = probs[u][:].rearrange("p (g m) -> p g m", m=WIN)
                nc.gpsimd.tensor_tensor(grid, grid, rinv[:, u, :].unsqueeze(2).broadcast_to([P, 16, WIN]),
                                        ALU.mult).then_inc(normed, 1)

            def split_cw(t):
                wait(pool, gate_step, at(t, GATE_STEPS, CW_FIRST))
                nc.gpsimd.tensor_tensor(cw_rest[:], cw[:], cw_parts[:, :, 0:ROUTED],
                                        ALU.subtract).then_inc(parts_step, 1)
                wait(pool, parts_step, at(t, 2, 1))
                nc.gpsimd.tensor_tensor(cw_parts[:, :, ROUTED:2 * ROUTED], cw_rest[:], zeros[:],
                                        ALU.add).then_inc(parts_step, 1)
                wait(pool, parts_step, at(t, 2, 2))
                nc.gpsimd.tensor_tensor(cw_parts[:, :, 2 * ROUTED:3 * ROUTED], cw_rest[:],
                                        cw_parts[:, :, ROUTED:2 * ROUTED], ALU.subtract).then_inc(cw_ready, 1)

            def attention(t, n):
                if n == STD1:
                    inverse_std(t + 1, mv1, ve1, rstd1, eps_conv, ln1_done, rstd1_step)
                if n == BIAS_X:
                    wait(pool, xres_loaded, at(t, 16, 16))
                    rows = x_res[:].rearrange("p (s c) -> p s c", s=SUBS)
                    nc.gpsimd.tensor_tensor(rows, rows, proj_b[:].unsqueeze(1).broadcast_to([P, SUBS, C]),
                                            ALU.add).then_inc(xres_biased, 1)
                if n == QS:
                    wait(pool, rotated, at(t, 4, 2))
                    nc.gpsimd.tensor_tensor(q_rot[:], q_rot[:], sines[:], ALU.add).then_inc(q_ready, 1)
                if n == KS:
                    wait(pool, rotated, at(t, 4, 4))
                    nc.gpsimd.tensor_tensor(k_rot[:], k_rot[:], sines[:], ALU.add).then_inc(k_ready, 1)
                for u in range(UNITS):
                    if n == (FIRST_NORMS if is_first(t) else NORMS)[u]:
                        normalise(t, u)
                if n == STD2:
                    inverse_std(t, mv2, ve2, rstd2, eps_ffn, ln2_done, rstd2_step)
                if n == X_LOW:
                    wait(pool, x_hi_ready, at(t, 1, 1))
                    nc.gpsimd.tensor_tensor(x_lo[:], xnT[:], x_hi[:].bitcast(F32), ALU.subtract).then_inc(x_lo_ready, 1)
                if n == GATE_END:
                    split_cw(t)

            def low_part(t, n):
                pool.wait_ge(hi_ready, at(t, CHUNKS, n + 1))
                nc.gpsimd.tensor_tensor(m_lo[n % RING][:], m[n % M_RING][:], m_hi[n % RING][:].bitcast(F32),
                                        ALU.subtract).then_inc(lo_by_pool, 1)

            def add(t, g):
                wait(pool, z_used, at(t, GROUPS, g + 1))
                if g > 1:
                    pool.wait_ge(y_added, at(t, ROUTED, g - 1))
                nc.gpsimd.tensor_tensor(y_sum[:], y_sum[:], weighted[g % 2][:], ALU.add).then_inc(y_added, 1)

            def weights_low(n):
                pool.wait_ge(w_hi_ready, n + 1)
                cols = slice(n * W_BLOCK, (n + 1) * W_BLOCK)
                nc.gpsimd.tensor_tensor(w_lo[:, cols], m[n % STAGES][:], w_hi[:, cols].bitcast(F32),
                                        ALU.subtract).then_inc(w_lo_ready, 1)

            def body(t, experts, attend):
                for n in range(STEPS):
                    if experts:
                        if 0 <= n - 1 < CHUNKS and (n - 1) % FC not in DVE_SHARE:
                            low_part(t, n - 1)
                        ended = n - LAG
                        if ended >= SH and ended % FC == FC - 1:
                            add(t, group(ended))
                    if attend:
                        attention(t, n)
                    for block_n in range(W_BLOCKS):
                        if not experts and n == W_STEPS[block_n]:
                            weights_low(block_n)

            nc.gpsimd.memset(half_neg[:], -0.5).then_inc(pool_fills, 1)
            nc.gpsimd.memset(eps_conv[:], EPS_CONV).then_inc(pool_fills, 1)
            nc.gpsimd.memset(eps_ffn[:], EPS_FFN).then_inc(pool_fills, 1)
            nc.gpsimd.memset(zeros[:], 0.0).then_inc(pool_fills, 1)
            nc.gpsimd.memset(v_spread[:], 0.0).then_inc(pool_fills, 1)
            nc.gpsimd.memset(cw_parts[:], 1.0).then_inc(pool_fills, 1)
            pool.wait_ge(pool_fills, POOL_FILLS)
            pool.sem_inc(lo_by_pool, POOL_LOWS)
            pool.sem_inc(y_added, ROUTED)
            inverse_std(0, mv1, ve1, rstd1, eps_conv, ln1_done, rstd1_step)
            pool.wait_ge(constants_in, 16 * SETUP_DMAS)
            run_iterations(pool, body)


def constants():
    ident = np.eye(P, dtype=np.float32)
    inv = (1.0 / np.float32(10000.0) ** (np.arange(0, HD // 2, 2, dtype=np.float32) / np.float32(HD // 2))).astype(np.float32)
    rows, cols = np.divmod(np.arange(WIN), 8)
    cos, sin = np.zeros((P, WIN), np.float32), np.zeros((P, WIN), np.float32)
    for ch in range(P):
        c = ch % HD
        pos = (rows if c < HD // 2 else cols).astype(np.float32)
        angle = pos * inv[(c % (HD // 2)) // 2]
        cos[ch] = np.cos(angle)
        sin[ch] = np.sin(angle) * (-1.0 if c % 2 == 0 else 1.0)
    headmask = (np.arange(P)[:, None] % 32 // HD == np.arange(HPR)[None]).astype(np.float32)
    e, j = np.meshgrid(np.arange(ROUTED), np.arange(ROUTED), indexing="ij")
    tiebreak = np.where(j < e, 0.0, MIN_NORMAL).astype(np.float32).reshape(-1)
    tiebreak = np.broadcast_to(np.tile(tiebreak, SUBS), (P, SUBS * ROUTED * ROUTED))
    const = np.concatenate([ident, cos, sin, headmask, tiebreak], axis=1)
    sel = np.zeros((CW_ROWS, ROUTED, P), np.float32)
    for part in range(3):
        for e in range(ROUTED):
            sel[part * ROUTED + e, e] = 1.0
    return np.ascontiguousarray(const), sel.reshape(CW_ROWS, ROUTED * P)


def windows(x):
    x = x.reshape(4, 2, 8, 2, 2, 8, 2, C)
    return x.transpose(0, 1, 4, 3, 6, 2, 5, 7).reshape(TOKENS, C)


def images(y):
    y = y.reshape(4, 2, 2, 2, 2, 8, 8, C)
    return y.transpose(0, 1, 5, 3, 2, 6, 4, 7).reshape(4, 32, 32, C)


def kernel(x, L0_conv_qkv_w, L0_conv_qkv_b, L0_conv_proj_w, L0_conv_proj_b, L0_ffn_gate_w, L0_ffn_gate_b,
           L0_ffn_sw1, L0_ffn_sb1, L0_ffn_sw2, L0_ffn_sb2, L0_ffn_rw1, L0_ffn_rb1, L0_ffn_rw2, L0_ffn_rb2):
    import concourse.bacc as _bacc
    from concourse.bass_utils import run_bass_kernel_spmd as _run

    A = np.asarray
    swap = np.arange(P).reshape(-1, 2)[:, ::-1].reshape(-1)
    qkv_w, qkv_b = A(L0_conv_qkv_w), A(L0_conv_qkv_b)
    q_w, k_w, v_w = qkv_w[0:P], qkv_w[P:2 * P], qkv_w[2 * P:]
    q_b, k_b, v_b = qkv_b[0:P], qkv_b[P:2 * P], qkv_b[2 * P:]
    const, sel = constants()
    w1 = np.concatenate([A(L0_ffn_sw1), A(L0_ffn_rw1)])
    w2 = np.concatenate([A(L0_ffn_sw2), A(L0_ffn_rw2)])
    b1 = np.concatenate([A(L0_ffn_sb1), A(L0_ffn_rb1)])
    up = w1.transpose(2, 0, 1).reshape(P, CHUNKS * P)
    down = w2.reshape(EXPERTS, C, FC, P).transpose(3, 0, 2, 1).reshape(P, CHUNKS * P)
    w12 = np.stack([up.reshape(P, EXPERTS, FC * P), down.reshape(P, EXPERTS, FC * P)], axis=2)
    w12 = w12.reshape(P, W_BLOCKS, W_BLOCK).transpose(1, 0, 2)
    b1 = b1.reshape(EXPERTS, FC, P).transpose(2, 0, 1).reshape(P, CHUNKS)
    arrays = {
        "x": windows(A(x)).reshape(TILES, SUBS, P, C).transpose(0, 2, 1, 3).reshape(TILES, P, TILE),
        "wqkv": np.concatenate([q_w.T, q_w[swap].T, k_w.T, k_w[swap].T, v_w.T, A(L0_conv_proj_w).T], axis=1),
        "bias": np.concatenate([q_b[:, None], q_b[swap][:, None], k_b[:, None], k_b[swap][:, None], v_b[:, None], b1],
                               axis=1),
        "const": const, "sel": sel,
        "proj_b": np.tile(A(L0_conv_proj_b), (P, 1)),
        "gate_w": A(L0_ffn_gate_w).T,
        "gate_b": np.tile(A(L0_ffn_gate_b), (P, SUBS)),
        "w12": w12,
        "b2": np.concatenate([np.tile(A(L0_ffn_rb2), (3, 1)), A(L0_ffn_sb2)]),
    }
    nc = _bacc.Bacc("TRN2", target_bir_lowering=False, num_devices=1)
    d, ins = {}, {}
    for name, a in arrays.items():
        ins[f"{name}_dram"] = a = np.ascontiguousarray(a)
        d[name] = nc.dram_tensor(f"{name}_dram", a.shape, mybir.dt.from_np(a.dtype), kind="ExternalInput").ap()
    d["yT"] = nc.dram_tensor("out_0_dram", (C, TOKENS), F32, kind="ExternalOutput").ap()
    build(nc, d)
    r = _run(nc, [ins], core_ids=[0])
    return images(r.results[0]["out_0_dram"].T)
```
